# Optimizing a Trainium2 kernel written in Bass

```python
import numpy as np
import jax
import jax.numpy as jnp

def _softmax(x, axis=-1):
    return jax.nn.softmax(x, axis=axis)

def _gelu(x):
    return jax.nn.gelu(x, approximate=True)

def _silu(x):
    return jax.nn.silu(x)

def _sigmoid(x):
    return jax.nn.sigmoid(x)

def _layernorm(x, axis=-1, eps=1e-05):
    m = jnp.mean(x, axis=axis, keepdims=True)
    v = jnp.var(x, axis=axis, keepdims=True)
    return (x - m) / jnp.sqrt(v + eps)

def _scatter_add(tgt, idx, src, axis=0):
    return tgt.at[idx].add(src)

def _segment_sum(src, seg, n):
    return jax.ops.segment_sum(src, seg, n)
kernel_name = 'mk_hybrid_d2_jaxref_r8_256fc8'

def setup_inputs(seed: int=0):
    np.random.seed(seed)
    _w = jnp.asarray

    def _L0_attn_a_setup():
        import jax, jax.numpy as jnp
        import numpy as np
        B, S, E = (4, 256, 128)
        H = 16
        D = E // H
        WIN = 64

        def _sliding_window_attention(q, k, v, win):
            b, h, s, d = q.shape
            nb = s // win
            scale = 1.0 / jnp.sqrt(jnp.float32(d))
            qb = q.reshape(b, h, nb, win, d)
            kb = k.reshape(b, h, nb, win, d)
            vb = v.reshape(b, h, nb, win, d)
            zpad = jnp.zeros_like(kb[:, :, :1])
            k2 = jnp.concatenate([jnp.concatenate([zpad, kb[:, :, :-1]], axis=2), kb], axis=3)
            v2 = jnp.concatenate([jnp.concatenate([zpad, vb[:, :, :-1]], axis=2), vb], axis=3)
            scores = jnp.einsum('bhnqd,bhnkd->bhnqk', qb, k2) * scale
            qi = jnp.arange(win)[:, None]
            kj = jnp.arange(2 * win)[None, :]
            delta = qi - kj + win
            valid = (delta >= 0) & (delta <= win)
            blk = jnp.arange(nb)[:, None, None]
            valid = valid[None] & (blk * win + (kj[None] - win) >= 0)
            slopes = jnp.exp2(-(jnp.arange(H, dtype=jnp.float32) + 1.0) * 8.0 / H)
            bias = slopes[:, None, None] * delta.astype(jnp.float32)
            scores = jnp.where(valid[None, :, :, :, :][:, None].squeeze(0)[None] if False else valid[None, None], scores + bias[None, :, None], -jnp.inf)
            p = jax.nn.softmax(scores, axis=-1)
            out = jnp.einsum('bhnqk,bhnkd->bhnqd', p, v2)
            return out.reshape(b, h, s, d)
        key = jax.random.key(seed)
        k1, k2, k3 = jax.random.split(key, 3)
        x = jax.random.normal(k1, (B, S, E), dtype=jnp.float32)
        w_in = jax.random.normal(k2, (3 * E, E), dtype=jnp.float32) * 0.02
        w_out = jax.random.normal(k3, (E, E), dtype=jnp.float32) * 0.02
        return {'x': x, 'w_in': w_in, 'w_out': w_out}
    _L0_attn_a_in = _L0_attn_a_setup()

    def _L0_attn_b_setup():
        import jax, jax.numpy as jnp
        import numpy as np
        D = 128
        H = 16
        KVH = 4
        HD = D // H
        LAT = 32
        WIN = 32
        B, S = (1, 256)
        BASE_G, BASE_L = (1000000.0, 10000.0)
        EPS = 1e-06

        def rmsnorm(x, w):
            return x * jax.lax.rsqrt(jnp.mean(x * x, axis=-1, keepdims=True) + EPS) * w

        def qk_norm(x):
            return x * jax.lax.rsqrt(jnp.mean(x * x, axis=-1, keepdims=True) + EPS)

        def rope(x, base):
            s, hd = (x.shape[-2], x.shape[-1])
            inv_freq = 1.0 / base ** (jnp.arange(0, hd, 2, dtype=jnp.float32) / hd)
            freqs = jnp.arange(s, dtype=jnp.float32)[:, None] * inv_freq[None, :]
            cos, sin = (jnp.cos(freqs), jnp.sin(freqs))
            xe, xo = (x[..., ::2], x[..., 1::2])
            out = jnp.stack([xe * cos - xo * sin, xe * sin + xo * cos], axis=-1)
            return out.reshape(x.shape)

        def split_heads(x, n_heads):
            b, s, _ = x.shape
            return x.reshape(b, s, n_heads, HD).transpose(0, 2, 1, 3)

        def repeat_kv(x):
            return jnp.repeat(x, H // KVH, axis=1)

        def sdpa(q, k, v, mask):
            scores = jnp.einsum('bhqd,bhkd->bhqk', q, k) / np.sqrt(HD).astype(np.float32)
            scores = jnp.where(mask, scores, jnp.float32(-1e+30))
            probs = jax.nn.softmax(scores, axis=-1)
            return jnp.einsum('bhqk,bhkd->bhqd', probs, v)

        def merge_heads(x):
            b, h, s, hd = x.shape
            return x.transpose(0, 2, 1, 3).reshape(b, s, h * hd)

        def global_latent_attn(x, wq, w_kv_down, w_k_up, w_v_up, wo):
            q = split_heads(x @ wq, H)
            latent = x @ w_kv_down
            k = split_heads(latent @ w_k_up, KVH)
            v = split_heads(latent @ w_v_up, KVH)
            q, k = (rope(q, BASE_G), rope(k, BASE_G))
            q, k = (qk_norm(q), qk_norm(k))
            k, v = (repeat_kv(k), repeat_kv(v))
            i = jnp.arange(x.shape[1])
            causal = i[:, None] >= i[None, :]
            return merge_heads(sdpa(q, k, v, causal)) @ wo

        def local_gqa_attn(x, wq, wk, wv, wo):
            q = split_heads(x @ wq, H)
            k = split_heads(x @ wk, KVH)
            v = split_heads(x @ wv, KVH)
            q, k = (rope(q, BASE_L), rope(k, BASE_L))
            q, k = (qk_norm(q), qk_norm(k))
            k, v = (repeat_kv(k), repeat_kv(v))
            i = jnp.arange(x.shape[1])
            diff = i[:, None] - i[None, :]
            mask = (diff >= 0) & (diff < WIN)
            return merge_heads(sdpa(q, k, v, mask)) @ wo
        key = jax.random.key(seed)
        ks = jax.random.split(key, 12)
        std = 0.02
        return {'hidden': jax.random.normal(ks[0], (B, S, D), dtype=jnp.float32), 'norm1_w': jnp.ones((D,), jnp.float32), 'norm2_w': jnp.ones((D,), jnp.float32), 'g_wq': jax.random.normal(ks[1], (D, H * HD), jnp.float32) * std, 'g_kv_down': jax.random.normal(ks[2], (D, LAT), jnp.float32) * std, 'g_k_up': jax.random.normal(ks[3], (LAT, KVH * HD), jnp.float32) * std, 'g_v_up': jax.random.normal(ks[4], (LAT, KVH * HD), jnp.float32) * std, 'g_wo': jax.random.normal(ks[5], (D, D), jnp.float32) * std, 'l_wq': jax.random.normal(ks[6], (D, H * HD), jnp.float32) * std, 'l_wk': jax.random.normal(ks[7], (D, KVH * HD), jnp.float32) * std, 'l_wv': jax.random.normal(ks[8], (D, KVH * HD), jnp.float32) * std, 'l_wo': jax.random.normal(ks[9], (D, D), jnp.float32) * std}
    _L0_attn_b_in = _L0_attn_b_setup()

    def _L0_ffn_setup():
        import jax, jax.numpy as jnp
        import numpy as np
        B, N, D = (4, 256, 128)
        SPARSITY = 0.01
        key = jax.random.key(seed)
        k1, k2, k3 = jax.random.split(key, 3)
        x = jax.random.normal(k1, (B, N, D), dtype=jnp.float32)
        spatial = jax.random.normal(k2, (D, D), dtype=jnp.float32) * 0.02
        freq = jnp.fft.fft(spatial, axis=-1)
        k = int(D * SPARSITY)
        mag = jnp.abs(freq)
        kth = jax.lax.top_k(mag, k)[0][:, -1:]
        w_sparse = jnp.where(mag >= kth, freq, 0.0 + 0j)
        bias = jax.random.normal(k3, (D,), dtype=jnp.float32) * 0.01
        return {'x': x, 'w_freq_real': jnp.real(w_sparse).astype(jnp.float32), 'w_freq_imag': jnp.imag(w_sparse).astype(jnp.float32), 'bias': bias}
    _L0_ffn_in = _L0_ffn_setup()

    def _L1_attn_a_setup():
        import jax, jax.numpy as jnp
        import numpy as np
        B, S, D = (8, 256, 128)
        EPS = 1e-07

        def _loc_weights(steps):
            idx = jnp.arange(steps)
            location = jnp.abs(idx[None, :] - idx[:, None]).astype(jnp.float32)
            lw = 1.0 / (location + EPS) * (location != 0).astype(jnp.float32)
            return lw
        key = jax.random.key(seed)
        kx, kw = jax.random.split(key)
        x = jax.random.normal(kx, (B, S, D), dtype=jnp.float32)
        limit = float(np.sqrt(6.0 / (D + D)))
        W = jax.random.uniform(kw, (D, D), dtype=jnp.float32, minval=-limit, maxval=limit)
        b = jnp.zeros((D,), dtype=jnp.float32)
        return {'x': x, 'W': W, 'b': b}
    _L1_attn_a_in = _L1_attn_a_setup()

    def _L1_attn_b_setup():
        import jax, jax.numpy as jnp
        import numpy as np
        B, S, H, NH = (2, 256, 128, 16)
        D = H // NH
        FF = 4 * H

        def _layernorm(x, g, b, eps=1e-05):
            mu = jnp.mean(x, axis=-1, keepdims=True)
            var = jnp.mean((x - mu) ** 2, axis=-1, keepdims=True)
            return (x - mu) * jax.lax.rsqrt(var + eps) * g + b

        def _attention(x, wq, bq, wk, bk, wv, bv, wo, bo):
            b, s, _ = x.shape
            q = (x @ wq.T + bq).reshape(b, s, NH, D).transpose(0, 2, 1, 3)
            k = (x @ wk.T + bk).reshape(b, s, NH, D).transpose(0, 2, 1, 3)
            v = (x @ wv.T + bv).reshape(b, s, NH, D).transpose(0, 2, 1, 3)
            scores = jnp.einsum('bhqd,bhkd->bhqk', q, k) / jnp.sqrt(jnp.float32(D))
            causal = jnp.tril(jnp.ones((s, s), jnp.float32))
            att = jax.nn.relu(scores) * causal
            att = att / (jnp.sum(att, axis=-1, keepdims=True) + 1e-09)
            ctx = jnp.einsum('bhqk,bhkd->bhqd', att, v)
            ctx = ctx.transpose(0, 2, 1, 3).reshape(b, s, H)
            return ctx @ wo.T + bo
        key = jax.random.key(seed)
        ks = jax.random.split(key, 20)

        def lin(k, o, i, scale=0.02):
            return jax.random.normal(k, (o, i), jnp.float32) * scale
        inp = {'x': jax.random.normal(ks[0], (B, S, H), jnp.float32), 'sf_w': lin(ks[1], H, H, 0.01), 'sf_b': jnp.zeros((H,), jnp.float32), 'mask': jax.random.bernoulli(ks[2], 0.1, (H, H)).astype(jnp.float32), 'wq': lin(ks[3], H, H), 'bq': jnp.zeros((H,), jnp.float32), 'wk': lin(ks[4], H, H), 'bk': jnp.zeros((H,), jnp.float32), 'wv': lin(ks[5], H, H), 'bv': jnp.zeros((H,), jnp.float32), 'wo': lin(ks[6], H, H), 'bo': jnp.zeros((H,), jnp.float32), 'ff1_w': lin(ks[7], FF, H), 'ff1_b': jnp.zeros((FF,), jnp.float32), 'ff2_w': lin(ks[8], H, FF), 'ff2_b': jnp.zeros((H,), jnp.float32), 'g1': jnp.ones((H,), jnp.float32), 'b1': jnp.zeros((H,), jnp.float32), 'g2': jnp.ones((H,), jnp.float32), 'b2': jnp.zeros((H,), jnp.float32), 'g3': jnp.ones((H,), jnp.float32), 'b3': jnp.zeros((H,), jnp.float32)}
        return inp
    _L1_attn_b_in = _L1_attn_b_setup()

    def _L1_ffn_setup():
        import jax, jax.numpy as jnp
        import numpy as np
        from jax import lax
        DIM = 128
        INTER = 64
        N_EXPERTS = 16
        TOPK = 4
        ROUTE_SCALE = 2.5
        VOCAB = 4000

        def _silu_and_mul(gu):
            gate, up = jnp.split(gu, 2, axis=-1)
            return jax.nn.silu(gate) * up
        key = jax.random.key(seed)
        ks = jax.random.split(key, 8)
        x = jax.random.normal(ks[0], (2, 64, DIM), dtype=jnp.float32)
        input_ids = jax.random.randint(ks[1], (2, 64), 0, VOCAB)
        s = 0.02
        gate_w = jax.random.normal(ks[2], (N_EXPERTS, DIM), dtype=jnp.float32) * s
        gate_b = jax.random.normal(ks[3], (N_EXPERTS,), dtype=jnp.float32) * s
        w13 = jax.random.normal(ks[4], (N_EXPERTS, 2 * INTER, DIM), dtype=jnp.float32) * s
        w2 = jax.random.normal(ks[5], (N_EXPERTS, DIM, INTER), dtype=jnp.float32) * s
        w13_s = jax.random.normal(ks[6], (2 * INTER, DIM), dtype=jnp.float32) * s
        w2_s = jax.random.normal(ks[7], (DIM, INTER), dtype=jnp.float32) * s
        return {'x': x, 'input_ids': input_ids, 'gate_w': gate_w, 'gate_b': gate_b, 'w13': w13, 'w2': w2, 'w13_s': w13_s, 'w2_s': w2_s}
    _L1_ffn_in = _L1_ffn_setup()
    _d = {'L0_attn_a_x': _L0_attn_a_in['x'], 'L0_attn_a_w_in': _L0_attn_a_in['w_in'], 'L0_attn_a_w_out': _L0_attn_a_in['w_out'], 'L0_attn_b_norm1_w': _L0_attn_b_in['norm1_w'], 'L0_attn_b_norm2_w': _L0_attn_b_in['norm2_w'], 'L0_attn_b_g_wq': _L0_attn_b_in['g_wq'], 'L0_attn_b_g_kv_down': _L0_attn_b_in['g_kv_down'], 'L0_attn_b_g_k_up': _L0_attn_b_in['g_k_up'], 'L0_attn_b_g_v_up': _L0_attn_b_in['g_v_up'], 'L0_attn_b_g_wo': _L0_attn_b_in['g_wo'], 'L0_attn_b_l_wq': _L0_attn_b_in['l_wq'], 'L0_attn_b_l_wk': _L0_attn_b_in['l_wk'], 'L0_attn_b_l_wv': _L0_attn_b_in['l_wv'], 'L0_attn_b_l_wo': _L0_attn_b_in['l_wo'], 'L0_ffn_w_freq_real': _L0_ffn_in['w_freq_real'], 'L0_ffn_w_freq_imag': _L0_ffn_in['w_freq_imag'], 'L0_ffn_bias': _L0_ffn_in['bias'], 'L1_attn_a_W': _L1_attn_a_in['W'], 'L1_attn_a_b': _L1_attn_a_in['b'], 'L1_attn_b_sf_w': _L1_attn_b_in['sf_w'], 'L1_attn_b_sf_b': _L1_attn_b_in['sf_b'], 'L1_attn_b_mask': _L1_attn_b_in['mask'], 'L1_attn_b_wq': _L1_attn_b_in['wq'], 'L1_attn_b_bq': _L1_attn_b_in['bq'], 'L1_attn_b_wk': _L1_attn_b_in['wk'], 'L1_attn_b_bk': _L1_attn_b_in['bk'], 'L1_attn_b_wv': _L1_attn_b_in['wv'], 'L1_attn_b_bv': _L1_attn_b_in['bv'], 'L1_attn_b_wo': _L1_attn_b_in['wo'], 'L1_attn_b_bo': _L1_attn_b_in['bo'], 'L1_attn_b_ff1_w': _L1_attn_b_in['ff1_w'], 'L1_attn_b_ff1_b': _L1_attn_b_in['ff1_b'], 'L1_attn_b_ff2_w': _L1_attn_b_in['ff2_w'], 'L1_attn_b_ff2_b': _L1_attn_b_in['ff2_b'], 'L1_attn_b_g1': _L1_attn_b_in['g1'], 'L1_attn_b_b1': _L1_attn_b_in['b1'], 'L1_attn_b_g2': _L1_attn_b_in['g2'], 'L1_attn_b_b2': _L1_attn_b_in['b2'], 'L1_attn_b_g3': _L1_attn_b_in['g3'], 'L1_attn_b_b3': _L1_attn_b_in['b3'], 'L1_ffn_input_ids': _L1_ffn_in['input_ids'], 'L1_ffn_gate_w': _L1_ffn_in['gate_w'], 'L1_ffn_gate_b': _L1_ffn_in['gate_b'], 'L1_ffn_w13': _L1_ffn_in['w13'], 'L1_ffn_w2': _L1_ffn_in['w2'], 'L1_ffn_w13_s': _L1_ffn_in['w13_s'], 'L1_ffn_w2_s': _L1_ffn_in['w2_s']}
    _x0 = _d['L0_attn_a_x']
    _d['L0_attn_a_x'] = jax.random.normal(jax.random.fold_in(jax.random.key(seed), 1), (2, 1024, 128), dtype=_x0.dtype)
    del _x0
    return _d

def reference(L0_attn_a_x, L0_attn_a_w_in, L0_attn_a_w_out, L0_attn_b_norm1_w, L0_attn_b_norm2_w, L0_attn_b_g_wq, L0_attn_b_g_kv_down, L0_attn_b_g_k_up, L0_attn_b_g_v_up, L0_attn_b_g_wo, L0_attn_b_l_wq, L0_attn_b_l_wk, L0_attn_b_l_wv, L0_attn_b_l_wo, L0_ffn_w_freq_real, L0_ffn_w_freq_imag, L0_ffn_bias, L1_attn_a_W, L1_attn_a_b, L1_attn_b_sf_w, L1_attn_b_sf_b, L1_attn_b_mask, L1_attn_b_wq, L1_attn_b_bq, L1_attn_b_wk, L1_attn_b_bk, L1_attn_b_wv, L1_attn_b_bv, L1_attn_b_wo, L1_attn_b_bo, L1_attn_b_ff1_w, L1_attn_b_ff1_b, L1_attn_b_ff2_w, L1_attn_b_ff2_b, L1_attn_b_g1, L1_attn_b_b1, L1_attn_b_g2, L1_attn_b_b2, L1_attn_b_g3, L1_attn_b_b3, L1_ffn_input_ids, L1_ffn_gate_w, L1_ffn_gate_b, L1_ffn_w13, L1_ffn_w2, L1_ffn_w13_s, L1_ffn_w2_s):

    def _L0_attn_a_ref(x, w_in, w_out):
        import jax, jax.numpy as jnp
        import numpy as np
        B, S, E = (4, 256, 128)
        H = 16
        D = E // H
        WIN = 64

        def _sliding_window_attention(q, k, v, win):
            b, h, s, d = q.shape
            nb = s // win
            scale = 1.0 / jnp.sqrt(jnp.float32(d))
            qb = q.reshape(b, h, nb, win, d)
            kb = k.reshape(b, h, nb, win, d)
            vb = v.reshape(b, h, nb, win, d)
            zpad = jnp.zeros_like(kb[:, :, :1])
            k2 = jnp.concatenate([jnp.concatenate([zpad, kb[:, :, :-1]], axis=2), kb], axis=3)
            v2 = jnp.concatenate([jnp.concatenate([zpad, vb[:, :, :-1]], axis=2), vb], axis=3)
            scores = jnp.einsum('bhnqd,bhnkd->bhnqk', qb, k2) * scale
            qi = jnp.arange(win)[:, None]
            kj = jnp.arange(2 * win)[None, :]
            delta = qi - kj + win
            valid = (delta >= 0) & (delta <= win)
            blk = jnp.arange(nb)[:, None, None]
            valid = valid[None] & (blk * win + (kj[None] - win) >= 0)
            slopes = jnp.exp2(-(jnp.arange(H, dtype=jnp.float32) + 1.0) * 8.0 / H)
            bias = slopes[:, None, None] * delta.astype(jnp.float32)
            scores = jnp.where(valid[None, :, :, :, :][:, None].squeeze(0)[None] if False else valid[None, None], scores + bias[None, :, None], -jnp.inf)
            p = jax.nn.softmax(scores, axis=-1)
            out = jnp.einsum('bhnqk,bhnkd->bhnqd', p, v2)
            return out.reshape(b, h, s, d)
        b, s, e = x.shape
        qkv = jnp.einsum('bse,fe->bsf', x, w_in)
        q, k, v = jnp.split(qkv, 3, axis=-1)

        def heads(t):
            return t.reshape(b, s, H, D).transpose(0, 2, 1, 3)
        o = _sliding_window_attention(heads(q), heads(k), heads(v), WIN)
        o = o.transpose(0, 2, 1, 3).reshape(b, s, e)
        return jnp.einsum('bse,fe->bsf', o, w_out)

    def _L0_attn_b_ref(hidden, norm1_w, norm2_w, g_wq, g_kv_down, g_k_up, g_v_up, g_wo, l_wq, l_wk, l_wv, l_wo):
        import jax, jax.numpy as jnp
        import numpy as np
        D = 128
        H = 16
        KVH = 4
        HD = D // H
        LAT = 32
        WIN = 32
        B, S = (1, 256)
        BASE_G, BASE_L = (1000000.0, 10000.0)
        EPS = 1e-06

        def rmsnorm(x, w):
            return x * jax.lax.rsqrt(jnp.mean(x * x, axis=-1, keepdims=True) + EPS) * w

        def qk_norm(x):
            return x * jax.lax.rsqrt(jnp.mean(x * x, axis=-1, keepdims=True) + EPS)

        def rope(x, base):
            s, hd = (x.shape[-2], x.shape[-1])
            inv_freq = 1.0 / base ** (jnp.arange(0, hd, 2, dtype=jnp.float32) / hd)
            freqs = jnp.arange(s, dtype=jnp.float32)[:, None] * inv_freq[None, :]
            cos, sin = (jnp.cos(freqs), jnp.sin(freqs))
            xe, xo = (x[..., ::2], x[..., 1::2])
            out = jnp.stack([xe * cos - xo * sin, xe * sin + xo * cos], axis=-1)
            return out.reshape(x.shape)

        def split_heads(x, n_heads):
            b, s, _ = x.shape
            return x.reshape(b, s, n_heads, HD).transpose(0, 2, 1, 3)

        def repeat_kv(x):
            return jnp.repeat(x, H // KVH, axis=1)

        def sdpa(q, k, v, mask):
            scores = jnp.einsum('bhqd,bhkd->bhqk', q, k) / np.sqrt(HD).astype(np.float32)
            scores = jnp.where(mask, scores, jnp.float32(-1e+30))
            probs = jax.nn.softmax(scores, axis=-1)
            return jnp.einsum('bhqk,bhkd->bhqd', probs, v)

        def merge_heads(x):
            b, h, s, hd = x.shape
            return x.transpose(0, 2, 1, 3).reshape(b, s, h * hd)

        def global_latent_attn(x, wq, w_kv_down, w_k_up, w_v_up, wo):
            q = split_heads(x @ wq, H)
            latent = x @ w_kv_down
            k = split_heads(latent @ w_k_up, KVH)
            v = split_heads(latent @ w_v_up, KVH)
            q, k = (rope(q, BASE_G), rope(k, BASE_G))
            q, k = (qk_norm(q), qk_norm(k))
            k, v = (repeat_kv(k), repeat_kv(v))
            i = jnp.arange(x.shape[1])
            causal = i[:, None] >= i[None, :]
            return merge_heads(sdpa(q, k, v, causal)) @ wo

        def local_gqa_attn(x, wq, wk, wv, wo):
            q = split_heads(x @ wq, H)
            k = split_heads(x @ wk, KVH)
            v = split_heads(x @ wv, KVH)
            q, k = (rope(q, BASE_L), rope(k, BASE_L))
            q, k = (qk_norm(q), qk_norm(k))
            k, v = (repeat_kv(k), repeat_kv(v))
            i = jnp.arange(x.shape[1])
            diff = i[:, None] - i[None, :]
            mask = (diff >= 0) & (diff < WIN)
            return merge_heads(sdpa(q, k, v, mask)) @ wo
        x = hidden
        x = x + global_latent_attn(rmsnorm(x, norm1_w), g_wq, g_kv_down, g_k_up, g_v_up, g_wo)
        x = x + local_gqa_attn(rmsnorm(x, norm2_w), l_wq, l_wk, l_wv, l_wo)
        return x

    def _L0_ffn_ref(x, w_freq_real, w_freq_imag, bias):
        import jax, jax.numpy as jnp
        import numpy as np
        B, N, D = (4, 256, 128)
        SPARSITY = 0.01
        w = jax.lax.complex(w_freq_real, w_freq_imag)
        x_freq = jnp.fft.fft(x, axis=-1)
        y_freq = jnp.einsum('bnd,do->bno', x_freq, w)
        y = jnp.real(jnp.fft.ifft(y_freq, axis=-1))
        return y + bias

    def _L1_attn_a_ref(x, W, b):
        import jax, jax.numpy as jnp
        import numpy as np
        B, S, D = (8, 256, 128)
        EPS = 1e-07

        def _loc_weights(steps):
            idx = jnp.arange(steps)
            location = jnp.abs(idx[None, :] - idx[:, None]).astype(jnp.float32)
            lw = 1.0 / (location + EPS) * (location != 0).astype(jnp.float32)
            return lw
        steps = x.shape[1]
        x_tran = jnp.matmul(x, W) + b
        weights = jnp.einsum('bsd,btd->bst', x_tran, x)
        lw = _loc_weights(steps)
        weights = jnp.exp(jnp.tanh(weights * lw))
        off_diag = 1.0 - jnp.eye(steps, dtype=weights.dtype)
        weights = weights * off_diag
        weights = weights / (jnp.sum(weights, axis=-1, keepdims=True) + EPS)
        return jnp.matmul(weights, x)

    def _L1_attn_b_ref(x, sf_w, sf_b, mask, wq, bq, wk, bk, wv, bv, wo, bo, ff1_w, ff1_b, ff2_w, ff2_b, g1, b1, g2, b2, g3, b3):
        import jax, jax.numpy as jnp
        import numpy as np
        B, S, H, NH = (2, 256, 128, 16)
        D = H // NH
        FF = 4 * H

        def _layernorm(x, g, b, eps=1e-05):
            mu = jnp.mean(x, axis=-1, keepdims=True)
            var = jnp.mean((x - mu) ** 2, axis=-1, keepdims=True)
            return (x - mu) * jax.lax.rsqrt(var + eps) * g + b

        def _attention(x, wq, bq, wk, bk, wv, bv, wo, bo):
            b, s, _ = x.shape
            q = (x @ wq.T + bq).reshape(b, s, NH, D).transpose(0, 2, 1, 3)
            k = (x @ wk.T + bk).reshape(b, s, NH, D).transpose(0, 2, 1, 3)
            v = (x @ wv.T + bv).reshape(b, s, NH, D).transpose(0, 2, 1, 3)
            scores = jnp.einsum('bhqd,bhkd->bhqk', q, k) / jnp.sqrt(jnp.float32(D))
            causal = jnp.tril(jnp.ones((s, s), jnp.float32))
            att = jax.nn.relu(scores) * causal
            att = att / (jnp.sum(att, axis=-1, keepdims=True) + 1e-09)
            ctx = jnp.einsum('bhqk,bhkd->bhqd', att, v)
            ctx = ctx.transpose(0, 2, 1, 3).reshape(b, s, H)
            return ctx @ wo.T + bo
        out = _layernorm(x, g1, b1)
        out = out @ (sf_w * mask).T + sf_b
        x = x + out
        out = _layernorm(x, g2, b2)
        out = _attention(out, wq, bq, wk, bk, wv, bv, wo, bo)
        x = x + out
        out = _layernorm(x, g3, b3)
        out = jax.nn.relu(out @ ff1_w.T + ff1_b)
        out = out @ ff2_w.T + ff2_b
        return x + out

    def _L1_ffn_ref(x, input_ids, gate_w, gate_b, w13, w2, w13_s, w2_s):
        import jax, jax.numpy as jnp
        import numpy as np
        from jax import lax
        DIM = 128
        INTER = 64
        N_EXPERTS = 16
        TOPK = 4
        ROUTE_SCALE = 2.5
        VOCAB = 4000

        def _silu_and_mul(gu):
            gate, up = jnp.split(gu, 2, axis=-1)
            return jax.nn.silu(gate) * up
        B, S, D = x.shape
        xt = x.reshape(-1, D)
        T = xt.shape[0]
        scores = jax.nn.sigmoid(xt.astype(jnp.float32) @ gate_w.T)
        biased = scores + gate_b
        _, idx = lax.top_k(biased, TOPK)
        w = jnp.take_along_axis(scores, idx, axis=-1)
        w = w / jnp.sum(w, axis=-1, keepdims=True)
        w = w * ROUTE_SCALE
        comb = jnp.zeros((T, N_EXPERTS), jnp.float32)
        comb = comb.at[jnp.arange(T)[:, None], idx].add(w)
        comb = comb.astype(x.dtype)

        def expert_body(y, args):
            w13_e, w2_e, c_e = args
            h = _silu_and_mul(xt @ w13_e.T)
            return (y + c_e[:, None] * (h @ w2_e.T), None)
        y, _ = lax.scan(expert_body, jnp.zeros_like(xt), (w13, w2, comb.T))
        y = y + _silu_and_mul(xt @ w13_s.T) @ w2_s.T
        return y.astype(x.dtype).reshape(B, S, D)
    x = L0_attn_a_x
    x = x + _L0_attn_a_ref(_layernorm(x, axis=-1), L0_attn_a_w_in, L0_attn_a_w_out)
    x = x + _L0_ffn_ref(_layernorm(x, axis=-1), L0_ffn_w_freq_real, L0_ffn_w_freq_imag, L0_ffn_bias)
    x = x + _L0_attn_b_ref(_layernorm(x, axis=-1), L0_attn_b_norm1_w, L0_attn_b_norm2_w, L0_attn_b_g_wq, L0_attn_b_g_kv_down, L0_attn_b_g_k_up, L0_attn_b_g_v_up, L0_attn_b_g_wo, L0_attn_b_l_wq, L0_attn_b_l_wk, L0_attn_b_l_wv, L0_attn_b_l_wo)
    x = x + _L0_ffn_ref(_layernorm(x, axis=-1), L0_ffn_w_freq_real, L0_ffn_w_freq_imag, L0_ffn_bias)
    x = x + _L1_attn_a_ref(_layernorm(x, axis=-1), L1_attn_a_W, L1_attn_a_b)
    x = x + _L1_ffn_ref(_layernorm(x, axis=-1), L1_ffn_input_ids, L1_ffn_gate_w, L1_ffn_gate_b, L1_ffn_w13, L1_ffn_w2, L1_ffn_w13_s, L1_ffn_w2_s)
    x = x + _L1_attn_b_ref(_layernorm(x, axis=-1), L1_attn_b_sf_w, L1_attn_b_sf_b, L1_attn_b_mask, L1_attn_b_wq, L1_attn_b_bq, L1_attn_b_wk, L1_attn_b_bk, L1_attn_b_wv, L1_attn_b_bv, L1_attn_b_wo, L1_attn_b_bo, L1_attn_b_ff1_w, L1_attn_b_ff1_b, L1_attn_b_ff2_w, L1_attn_b_ff2_b, L1_attn_b_g1, L1_attn_b_b1, L1_attn_b_g2, L1_attn_b_b2, L1_attn_b_g3, L1_attn_b_b3)
    x = x + _L1_ffn_ref(_layernorm(x, axis=-1), L1_ffn_input_ids, L1_ffn_gate_w, L1_ffn_gate_b, L1_ffn_w13, L1_ffn_w2, L1_ffn_w13_s, L1_ffn_w2_s)
    return x

_drawn_inputs = setup_inputs


def setup_inputs(seed=0):
    import zlib

    import numpy as np

    out = dict(_drawn_inputs(seed))
    spreads = {'L0_attn_b_norm1_w': (1.0, 0.6),
     'L0_attn_b_norm2_w': (1.0, 0.6),
     'L1_attn_a_b': (0.0, 2.0),
     'L1_attn_b_sf_b': (0.0, 0.283),
     'L1_attn_b_bq': (0.0, 0.8),
     'L1_attn_b_bk': (0.0, 0.8),
     'L1_attn_b_bv': (0.0, 0.8),
     'L1_attn_b_bo': (0.0, 0.279),
     'L1_attn_b_ff1_b': (0.0, 0.8),
     'L1_attn_b_ff2_b': (0.0, 0.1),
     'L1_attn_b_g1': (1.0, 0.6),
     'L1_attn_b_b1': (0.0, 0.8),
     'L1_attn_b_g2': (1.0, 0.6),
     'L1_attn_b_b2': (0.0, 0.8),
     'L1_attn_b_g3': (1.0, 0.6),
     'L1_attn_b_b3': (0.0, 0.8)}
    factors = {'L0_attn_a_w_in': 3.806,
     'L0_attn_a_w_out': 3.7,
     'L0_attn_b_g_wq': 8.0,
     'L0_attn_b_g_kv_down': 8.0,
     'L0_attn_b_g_k_up': 8.0,
     'L0_attn_b_g_v_up': 8.0,
     'L0_attn_b_g_wo': 8.0,
     'L0_attn_b_l_wq': 8.0,
     'L0_attn_b_l_wk': 8.0,
     'L0_attn_b_l_wv': 8.0,
     'L0_attn_b_l_wo': 8.0,
     'L0_ffn_bias': 3.066,
     'L1_attn_a_W': 8.0,
     'L1_attn_b_sf_w': 4.591,
     'L1_attn_b_wq': 8.0,
     'L1_attn_b_wk': 8.0,
     'L1_attn_b_wv': 8.0,
     'L1_attn_b_wo': 7.511,
     'L1_attn_b_ff1_w': 2.877,
     'L1_ffn_gate_w': 8.0,
     'L1_ffn_gate_b': 8.0,
     'L1_ffn_w13': 8.0,
     'L1_ffn_w2': 8.0,
     'L1_ffn_w13_s': 8.0,
     'L1_ffn_w2_s': 8.0}
    for name, (base, spread) in spreads.items():
        noise = np.random.default_rng([zlib.crc32(name.encode()), seed]).standard_normal(out[name].shape)
        drawn = base * np.exp(spread * noise) if base else spread * noise
        out[name] = jnp.asarray(drawn.astype(out[name].dtype))
    for name, factor in factors.items():
        out[name] = (out[name] * factor).astype(out[name].dtype)
    return out
```

```python
from contextlib import ExitStack

import numpy as np

import concourse.bass as bass
from concourse import mybir

F32 = mybir.dt.float32
BF16 = mybir.dt.bfloat16
BF16_NP = mybir.dt.np(BF16)
ALU = mybir.AluOpType
ACT = mybir.ActivationFunctionType
AX = mybir.AxisListType

B, S, E = 2, 1024, 128
T = B * S
CH = 512
NC = T // CH
CB = S // CH
P = 128
H, D = 16, E // 16
KVH = 4
G = 4
NG = H // G
KT = S // P
VW = 2 * D
ROWS = 9 * D
PAD = 64
SL = S + PAD
XROWS = 16
WIN_A, WIN_L = 64, 32
W_A, W_L = P + WIN_A, P + WIN_L
NEG = -1e30
SCALE = float(1.0 / np.sqrt(np.float32(D)))
NE, INTER, TOPK = 16, 64, 4
ROUTE = 2.5
NPAIR = NE // 2
FF = 4 * E
NORMS = 13
LANE = 20

AW, AG, AL, AR = 0, 1, 2, 3
GQA = (False, True, True, False)
ROPE = (False, True, True, False)
U_AW, U_F0, U_AG, U_AL, U_F1, U_LOC, U_M0, U_SF, U_AR, U_FF, U_M1 = range(11)
R_AW, R_AG, R_AL, R_LOC, R_AR = range(5)
RECIP_OF = {AW: R_AW, AG: R_AG, AL: R_AL, AR: R_AR}

WCOLS = [
    ("a_wq", 128), ("a_wk", 128), ("a_wv", 128), ("a_wo", 128),
    ("g_wq", 128), ("g_wqr", 128), ("g_wo", 128), ("g_kvd", 128), ("g_kup", 32), ("g_kupr", 32), ("g_vup", 32),
    ("l_wq", 128), ("l_wqr", 128), ("l_wk", 32), ("l_wkr", 32), ("l_wv", 32), ("l_wo", 128),
    ("f_re", 128), ("f_im", 128), ("loc_w", 128),
    ("sf_w", 128), ("sf_m", 128), ("r_wq", 128), ("r_wk", 128), ("r_wv", 128), ("r_wo", 128), ("r_bv", 128),
    ("ff1", FF), ("ff2", FF), ("gate_w", NE), ("gate_b", NE),
    ("w_gate", NPAIR * 128 + INTER), ("w_up", NPAIR * 128 + INTER), ("w_down", NPAIR * 128 + 128),
]
VCOLS = ["n1", "n2", "f_b", "loc_b", "sf_b", "r_bq", "r_bk", "r_bo", "ff1_b0", "ff1_b1", "ff1_b2", "ff1_b3",
         "ff2_b", "g1", "b1", "g2", "b2", "g3", "b3"]
CCOLS = [("dft_c", 128), ("dft_s", 128), ("dft_ns", 128), ("idft_c", 128), ("idft_ns", 128), ("ident", 128),
         ("center", 128), ("mean", 128), ("ones", 128), ("head_q", 128), ("head_k", 32), ("offdiag", 128),
         ("near", P * (2 * KT - 1))]
BCOLS = [("ident", 128), ("band_q", 2 * W_A), ("band_a", 2 * W_A), ("band_l", 2 * W_L), ("causal", 128),
         ("spread", NPAIR * 128)]


def columns(spec):
    at, out = 0, {}
    for name, n in spec:
        out[name] = (at, at + n)
        at += n
    return out, at


WAT, WN = columns(WCOLS)
CAT, CN = columns(CCOLS)
BAT, BN = columns(BCOLS)
VAT = {name: i for i, name in enumerate(VCOLS)}


def build(nc, xt, wp, vp, cp, bp, rope_q, rope_k, bias_q, bias_k, out):
    ctx = ExitStack()
    with ctx:
        def sb(name, shape, dt):
            return ctx.enter_context(nc.sbuf_tensor(name, shape, dt))

        def sem(name):
            return ctx.enter_context(nc.semaphore(name))

        x = sb("x", [P, T], F32)
        h = sb("h", [P, T], F32)
        z = sb("z", [P, T], F32)
        wsb = sb("wsb", [P, WN], F32)
        vsb = sb("vsb", [P, len(VCOLS)], F32)
        csb = sb("csb", [P, CN], F32)
        bsb = sb("bsb", [P, BN], BF16)
        eps = sb("eps", [P, 2], F32)
        fm = sb("fm", [P, 128], F32)
        g_kv = sb("g_kv", [P, 96], F32)
        ropeq = sb("ropeq", [P, 2, S], F32)
        ropek = sb("ropek", [KVH * D, 2, S], F32)
        nsq = sb("nsq", [P, NC, CH], F32)
        nrr = sb("nrr", [P, NC, CH], F32)
        vf = sb("vf", [P, B * KT, H, VW], F32)
        aux = sb("aux", [P, 6 * CH], F32)
        mxq = sb("mxq", [P, B, G * KT], F32)
        mxt = sb("mxt", [G * KT, B, 2, P], F32)
        mxp = sb("mxp", [G * KT, B, 3, P], BF16)
        stf = sb("stf", [P, B * G * (S + SL) // 2], F32)
        work = sb("work", [P, 16 * CH], F32)
        qst = stf[:, 0:B * G * S // 2].bitcast(BF16).rearrange("p (b g s) -> p b g s", b=B, g=G)
        kst = stf[:, B * G * S // 2:].bitcast(BF16).rearrange("p (b g s) -> p b g s", b=B, g=G)
        oev = aux[:, 0:4 * CH].rearrange("p (b s) -> p b s", b=B)
        vg = aux[:, 4 * CH:6 * CH].rearrange("p (b t g v) -> p b t g v", b=B, t=KT, g=G)
        prob = work[:].rearrange("p (s g w) -> p s g w", s=2, g=G)
        wbf = work[:, 0:12 * CH].bitcast(BF16).rearrange("p (t b i s) -> p t b i s", t=2, b=B, i=3)
        qf = work[:, 12 * CH:14 * CH].rearrange("p (m s) -> p m s", m=2)
        rem = work[:, 14 * CH:16 * CH].rearrange("p (m s) -> p m s", m=2)
        rope_t = aux[:].rearrange("p (m k s) -> p m k s", m=2, k=3)
        ot = stf[:, 0:T]
        dt_ = stf[:, T:2 * T]
        rcp = work[:, 0:12 * CH].rearrange("p (k c s) -> p k c s", k=3, c=NC)
        xtr = stf[:, 0:T]
        zr = stf[:, T:2 * T].rearrange("p (t d) -> p t d", t=B * KT)
        dacc = stf[:, 2 * T:3 * T]
        dloc = stf[:, 3 * T:4 * T]
        comb = stf[:, 0:T // 2].bitcast(BF16)
        moe = work[:, 0:12 * CH].rearrange("p (k m s) -> p k m s", k=6, m=2)
        rt = stf[:, T:T + 2048]
        ffh = work[:, 0:8 * CH].rearrange("p (m k s) -> p m k s", m=2, k=4)

        ps = ctx.enter_context(nc.psum_tensor("ps", [P, 8, CH], F32))

        def bank(i):
            return ps[:, i, :]

        def two(i):
            return ps[:, i:i + 2, :].rearrange("p a s -> p (a s)")

        def w_(name, rows=P):
            a, b = WAT[name]
            return wsb[0:rows, a:b]

        def c_(name, rows=P):
            a, b = CAT[name]
            return csb[0:rows, a:b]

        def b_(name):
            a, b = BAT[name]
            return bsb[:, a:b]

        def v_(name, rows=P):
            return vsb[0:rows, VAT[name]:VAT[name] + 1]

        def ch(t, c):
            return t[:, c * CH:(c + 1) * CH]

        scr_q = nc.dram_tensor("scr_q", (9, P, T), BF16, kind="Internal").ap()
        scr_k = nc.dram_tensor("scr_k", (9, P, T), BF16, kind="Internal").ap()
        scr_kg = nc.dram_tensor("scr_kg", (9, KVH * D, T), BF16, kind="Internal").ap()
        scr_o = nc.dram_tensor("scr_o", (NG, P, T), F32, kind="Internal").ap()

        s_x = sem("x_loaded")
        s_w = sem("weights_loaded")
        s_cst = sem("constants_loaded")
        s_rope = sem("rope_loaded")
        s_set = sem("memory_set")
        s_zero = sem("stack_rows_zeroed")
        s_fa = sem("fourier_a")
        s_fb = sem("fourier_b")
        n_cen = sem("norm_centered")
        n_sq = sem("norm_squared")
        n_var = sem("norm_variance")
        n_ln = sem("norm_log")
        n_r = sem("norm_factor")
        n_half = sem("norm_scaled")
        n_z = sem("norm_done")
        s_lin = sem("layer_out")
        s_res = sem("residual_done")
        s_mid = sem("residual_mid")
        p_mm = sem("proj_in_psum")
        p_t = sem("rope_products")
        p_rot = sem("rope_sum")
        p_sq = sem("head_squares")
        p_var = sem("head_variance")
        p_ln = sem("head_log")
        p_r = sem("head_factor")
        p_f = sem("proj_float")
        p_fn = sem("proj_normed")
        p_1 = sem("part_1")
        p_r1 = sem("rest_1")
        p_2 = sem("part_2")
        p_3 = sem("part_3")
        p_v = sem("values_in_psum")
        p_vf = sem("values_copied")
        s_scr = sem("parts_stored")
        s_ol = [sem(f"attention_out_loaded{b}") for b in range(B)]
        d_add = sem("denominator_guarded")
        d_ln = sem("denominator_log")
        d_0 = sem("reciprocal_guess")
        d_u = sem("reciprocal_product")
        d_v = sem("reciprocal_done")
        d_o = sem("attention_normed")
        l_xt = sem("loc_transformed")
        l_xc = sem("loc_transformed_copied")
        l_tr = sem("loc_transposed")
        l_tc = sem("loc_transposed_copied")
        l_s = sem("loc_scores")
        l_w = sem("loc_weighted")
        l_th = sem("loc_tanh")
        l_e = sem("loc_exp")
        l_p = sem("loc_diagonal_cleared")
        l_acc = sem("loc_sum")
        l_pv = sem("loc_values")
        l_den = sem("loc_denominator")
        m_log = sem("route_logits")
        m_e = sem("route_exp")
        m_d = sem("route_step")
        m_t = sem("route_transposed")
        m_c = sem("route_part")
        m_cs = sem("route_stack")
        m_gu = sem("expert_gate_up")
        m_sg = sem("expert_silu")
        m_su = sem("expert_product")
        m_h = sem("expert_hidden")
        m_y = sem("expert_down")
        f_h = sem("ff_hidden_in_psum")
        f_r = sem("ff_hidden")
        s_out = sem("out_stored")

        A = []
        for a, tag in enumerate(("win", "glob", "loc", "relu")):
            A.append(dict(
                stack=[sem(f"{tag}_stack_loaded{b}") for b in range(B)],
                vg=[sem(f"{tag}_values_ready{b}") for b in range(B)],
                unit=[sem(f"{tag}_unit{i}") for i in range(3)],
                soft=[sem(f"{tag}_probs{i}") for i in range(3)],
                pv=[sem(f"{tag}_pv{i}") for i in range(2)],
                oev=[sem(f"{tag}_out_copied{b}") for b in range(B)],
                st=[sem(f"{tag}_out_stored{b}") for b in range(B)],
            ))
        w_s = [sem(f"max_scores{i}") for i in range(2)]
        w_m = [sem(f"max_taken{i}") for i in range(2)]
        w_t = sem("max_transposed")
        w_n = sem("max_step")
        w_l = [sem(f"max_rows_loaded{b}") for b in range(B)]

        block = ctx.enter_context(nc.Block())

        def nrm(n):
            return [
                (x, z, "ln", None, None, (s_x, None)),
                (x, z, "ln", None, None, (s_res, U_AW)),
                (x, h, "ln", None, None, (s_res, U_F0)),
                (h, z, "rms", "n1", None, (n_z, 2)),
                (h, z, "rms", "n2", None, (s_res, U_AG)),
                (x, z, "ln", None, None, (s_res, U_AL)),
                (x, z, "ln", None, None, (s_res, U_F1)),
                (x, z, "ln", None, None, (s_res, U_LOC)),
                (x, h, "ln", None, None, (s_res, U_M0)),
                (h, z, "ln", "g1", "b1", (n_z, 8)),
                (h, z, "ln", "g2", "b2", (s_res, U_SF)),
                (h, z, "ln", "g3", "b3", (s_res, U_AR)),
                (x, z, "ln", None, None, (s_res, U_FF)),
            ][n]

        N_OF = {AW: 0, AG: 3, AL: 4, AR: 10}

        def wait_source(eng, n, c):
            s, k = nrm(n)[5]
            eng.wait_ge(s, 16 * NC if k is None else 4 * k + c + 1)

        def outputs(u, c):
            return 4 * (u - (u > U_LOC)) + c + 1

        def pieces(step, g):
            if step < 4:
                return [(step, P * step, P * step, CH), (step, CH, CH, S)]
            if step == 4:
                return [(5, 5 * P, 0, 3 * P), (7, 7 * P, 3 * P, 4 * P), (4, 4 * P, CH, S)]
            return [(6, 6 * P, 2 * P * g, 2 * P * g + 2 * P)]

        STEPS = 6
        UNITS = 5 * G + 1

        @block.sync
        def _(sp):
            for c in range(NC):
                sp.dma_start(ch(x, c), xt[:, c * CH:(c + 1) * CH]).then_inc(s_x, 16)
            sp.dma_start(csb[:], cp).then_inc(s_cst, 16)
            sp.dma_start(bsb[:], bp).then_inc(s_cst, 16)
            sp.dma_start(vsb[:], vp).then_inc(s_cst, 16)
            half = WAT["g_wq"][0]
            sp.dma_start(wsb[:, 0:half], wp[:, 0:half]).then_inc(s_w, 16)
            sp.dma_start(wsb[:, half:WN], wp[:, half:WN]).then_inc(s_w, 16)

            def rope_load(i):
                sp.dma_start(ropeq[:], rope_q[i].rearrange("k p s -> p k s")).then_inc(s_rope, 16)
                sp.dma_start(ropek[:], rope_k[i].rearrange("k p s -> p k s")).then_inc(s_rope, 16)

            def store_parts(a):
                for b in range(B):
                    for t in range(2):
                        rows = KVH * D if t and GQA[a] else P
                        dst = scr_q if t == 0 else (scr_kg if GQA[a] else scr_k)
                        for i in range(3):
                            done = 8 * a + 2 * (CB * b + CB - 1) + t + 1
                            sp.wait_ge([p_1, p_2, p_3][i], done)
                            slots = dst[3 * i:3 * i + 3] if t == 0 else dst[i:9:3]
                            src = wbf[0:rows, t, b, i].unsqueeze(1).broadcast_to([rows, 3, S])
                            sp.dma_start(slots[:, :, b * S:(b + 1) * S].rearrange("r p s -> p r s"),
                                         src).then_inc(s_scr, 16)
                sp.wait_ge(s_scr, 16 * 12 * (a + 1))

            def load_stacks(a, g, b):
                q = A[a]
                src = scr_q.rearrange("r (d h) s -> (r d) h s", h=H)[:, bass.ds(G * g, G), b * S:(b + 1) * S]
                sp.dma_start(qst[0:ROWS, b], src).then_inc(q["stack"][b], 16)
                if GQA[a]:
                    src = scr_kg.rearrange("r (d h) s -> (r d) h s", h=KVH)[:, bass.ds(g, 1), b * S:(b + 1) * S]
                    sp.dma_start(kst[0:ROWS, b, 0:1, PAD:SL], src).then_inc(q["stack"][b], 16)
                else:
                    src = scr_k.rearrange("r (d h) s -> (r d) h s", h=H)[:, bass.ds(G * g, G), b * S:(b + 1) * S]
                    sp.dma_start(kst[0:ROWS, b, :, PAD:SL], src).then_inc(q["stack"][b], 16)
                if a == AW:
                    sp.dma_start(qst[ROWS:ROWS + XROWS, b], bias_q[:, bass.ds(G * g, G), :])\
                      .then_inc(q["stack"][b], 16)
                    sp.dma_start(kst[ROWS:ROWS + XROWS, b], bias_k[:, bass.ds(G * g, G), :])\
                      .then_inc(q["stack"][b], 16)

            def load_max(g, b):
                sp.wait_ge(w_n, 4 * (2 * g + b + 1))
                for i in range(3):
                    r = ROWS + XROWS - 3 + i
                    sp.dma_start(qst[r:r + 1, b].rearrange("p g s -> p (g s)"), mxp[:, b, i, :]).then_inc(w_l[b], 16)

            def store_out(a, g, b):
                q = A[a]
                sp.wait_ge(q["oev"][b], g + 2)
                sp.dma_start(scr_o[bass.ds(g, 1), :, b * S:(b + 1) * S].rearrange("g p s -> (g p) s"),
                             oev[:, b, :]).then_inc(q["st"][b], 16)

            def attention(a):
                q = A[a]
                store_parts(a)
                for b in range(B):
                    sp.sem_inc(q["st"][b], 16)
                if a == AW:
                    sp.wait_ge(s_set, 1)
                else:
                    sp.wait_ge(s_zero, a)
                for b in range(B):
                    load_stacks(a, 0, b)

                def body(g, last):
                    if a == AW:
                        load_max(g, 0)
                        load_max(g, 1)
                    for b in range(B):
                        store_out(a, g, b)
                        if not last:
                            if a in (AW, AL):
                                sp.wait_ge(q["unit"][1], 8 * g + 4 * b + 4)
                            else:
                                sp.wait_ge(q["unit"][2], 14 * g + 7 * b + 7)
                            load_stacks(a, g + 1, b)

                with sp.Fori(0, NG - 1) as g:
                    body(g, False)
                body(NG - 1, True)
                for b in range(B):
                    sp.wait_ge(q["st"][b], 16 * (NG + 1))
                    for k, t in enumerate((ot, dt_)):
                        src = scr_o.rearrange("g (q r) s -> (g q) r s", q=G)[:, k * D:(k + 1) * D, b * S:(b + 1) * S]
                        sp.dma_start(t[:, b * S:(b + 1) * S], src).then_inc(s_ol[b], 16)

            attention(AW)
            rope_load(0)
            attention(AG)
            sp.wait_ge(p_t, 8)
            rope_load(1)
            attention(AL)
            attention(AR)
            for c in range(NC):
                sp.wait_ge(s_res, 4 * U_M1 + c + 1)
                sp.dma_start(out[:, c * CH:(c + 1) * CH], ch(x, c)).then_inc(s_out, 16)
            sp.wait_ge(s_out, 16 * NC)

        @block.gpsimd
        def _(pool):
            def rest_of(a):
                for c in range(NC):
                    for t in range(2):
                        m = 2 * c + t
                        k = 8 * a + m
                        r = KVH * D if t and GQA[a] else P
                        rt_ = rope_t[0:r, m % 2]
                        if ROPE[a]:
                            kr = k - 8
                            pool.wait_ge(p_3, k)
                            pool.wait_ge(p_t, kr + 1)
                            nc.gpsimd.tensor_tensor(rt_[:, 0], rt_[:, 0], rt_[:, 1], ALU.add).then_inc(p_rot, 1)
                            pool.wait_ge(p_r, kr + 1)
                            nc.gpsimd.tensor_tensor(qf[0:r, m % 2], rt_[:, 0], rt_[:, 2], ALU.mult)\
                                .then_inc(p_fn, 1)
                        pool.wait_ge(p_1, k + 1)
                        part = wbf[0:r, t, c // CB, :, (c % CB) * CH:(c % CB + 1) * CH]
                        nc.gpsimd.tensor_tensor(rem[0:r, m % 2], qf[0:r, m % 2], part[:, 0], ALU.subtract)\
                            .then_inc(p_r1, 1)
                        pool.wait_ge(p_2, k + 1)
                        nc.gpsimd.tensor_tensor(part[:, 2], rem[0:r, m % 2], part[:, 1], ALU.subtract)\
                            .then_inc(p_3, 1)

            def group_values(a):
                q = A[a]
                pool.wait_ge(p_vf, 4 * (a + 1))
                pool.wait_ge(p_3, 8 * (a + 1))
                nvh, nh = (1, 1) if GQA[a] else (G, G)
                with pool.Fori(0, NG) as g:
                    for b in range(B):
                        pool.wait_ge(q["oev"][b], g + 1)
                        nc.gpsimd.tensor_copy(vg[:, b, :, 0:nh, :],
                                              vf[:, b * KT:(b + 1) * KT, bass.ds(nvh * g, nvh), :])\
                            .then_inc(q["vg"][b], 1)

            def reciprocal(i):
                for c in range(NC):
                    d = ch(dloc if i == R_LOC else dt_, c)
                    pool.wait_ge(d_0, 4 * i + c + 1)
                    nc.gpsimd.tensor_tensor(rcp[:, 1, c], d, rcp[:, 0, c], ALU.mult).then_inc(d_u, 1)

            def attention(a):
                if a != AW:
                    pool.wait_ge(s_res, 4 * {AG: U_AW, AL: U_AG, AR: U_M0}[a] + 4)
                    nc.gpsimd.memset(stf[64:P, :], 0.0).then_inc(s_zero, 1)
                    pool.wait_ge(s_zero, a)
                rest_of(a)
                group_values(a)
                reciprocal(RECIP_OF[a])

            pool.wait_ge(s_cst, 48)
            attention(AW)
            attention(AG)
            attention(AL)
            for v in range(B * KT):
                t = v % KT
                blk = work[:, (4 + v % 2) * S + t * P:(4 + v % 2) * S + (t + 1) * P]
                pool.wait_ge(l_e, v + 1)
                nc.gpsimd.tensor_tensor(blk, blk, c_("offdiag"), ALU.mult).then_inc(l_p, 1)
            reciprocal(R_LOC)
            attention(AR)

        @block.scalar
        def _(act):
            def norm(n):
                src, _, kind, _, _, _ = nrm(n)
                for c in range(NC):
                    i = 4 * n + c
                    if kind == "ln":
                        act.wait_ge(n_cen, i + 1 - 4 * (n > 3) - 4 * (n > 4))
                        nc.scalar.activation(nsq[:, c], bank(c), ACT.Square).then_inc(n_sq, 1)
                    else:
                        wait_source(act, n, c)
                        nc.scalar.activation(nsq[:, c], ch(src, c), ACT.Square).then_inc(n_sq, 1)
                e = eps[:, 0:1] if kind == "ln" else eps[:, 1:2]
                for c in range(NC):
                    i = 4 * n + c
                    act.wait_ge(n_var, i + 1)
                    nc.scalar.activation(nrr[:, c], bank(4 + c), ACT.Ln, bias=e).then_inc(n_ln, 1)
                    act.wait_ge(n_ln, i + 1)
                    nc.scalar.activation(nrr[:, c], nrr[:, c], ACT.Exp, scale=-0.5).then_inc(n_r, 1)

            def parts_of(a):
                for c in range(NC):
                    for t in range(2):
                        m = 2 * c + t
                        k = 8 * a + m
                        r = KVH * D if t and GQA[a] else P
                        if a == AW:
                            act.wait_ge(p_mm, k + 1)
                            if m >= 2:
                                act.wait_ge(p_r1, k - 1)
                            nc.scalar.activation(qf[:, m % 2], bank(c + 4 * t), ACT.Copy).then_inc(p_f, 1)
                            act.wait_ge(p_f, m + 1)
                        elif a == AR:
                            act.wait_ge(p_mm, k + 1)
                            if m >= 2:
                                act.wait_ge(p_r1, k - 1)
                            nc.scalar.activation(qf[:, m % 2], bank(c + 4 * t), ACT.Identity,
                                                 bias=v_("r_bk" if t else "r_bq")).then_inc(p_f, 1)
                            act.wait_ge(p_f, 8 + m + 1)
                        else:
                            kr = k - 8
                            rt_ = rope_t[0:r, m % 2]
                            act.wait_ge(p_rot, kr + 1)
                            nc.scalar.activation(rt_[:, 1], rt_[:, 0], ACT.Square).then_inc(p_sq, 1)
                            act.wait_ge(p_var, kr + 1)
                            nc.scalar.activation(rt_[:, 2], ps[0:r, c, :], ACT.Ln, bias=eps[0:r, 1:2])\
                                .then_inc(p_ln, 1)
                            act.wait_ge(p_ln, kr + 1)
                            nc.scalar.activation(rt_[:, 2], rt_[:, 2], ACT.Exp, scale=-0.5).then_inc(p_r, 1)
                            act.wait_ge(p_fn, kr + 1)
                        part = wbf[0:r, t, c // CB, :, (c % CB) * CH:(c % CB + 1) * CH]
                        nc.scalar.activation(part[:, 0], qf[0:r, m % 2], ACT.Copy).then_inc(p_1, 1)
                        act.wait_ge(p_r1, k + 1)
                        nc.scalar.activation(part[:, 1], rem[0:r, m % 2], ACT.Copy).then_inc(p_2, 1)

            def band_soft(a):
                q = A[a]
                w = W_A if a == AW else W_L
                for i in range(2):
                    act.sem_inc(q["soft"][i], 1)
                with act.Fori(0, NG) as g:
                    for b in range(B):
                        for st in range(2):
                            act.wait_ge(q["pv"][st], 2 * g + b + 1)
                            for g4 in range(G):
                                k = G * st + g4
                                act.wait_ge(q["unit"][k % 2], 8 * g + 4 * b + k // 2 + 1)
                                src = ps[:, 2 * (k % 2):2 * (k % 2) + 2, 0:2 * w]
                                dst = prob[:, st, g4].rearrange("p (a s) -> p a s", a=2)[:, :, 0:2 * w]
                                nc.scalar.activation(dst, src, ACT.Exp, scale=SCALE).then_inc(q["soft"][k % 2], 1)

            def full_soft(a):
                q = A[a]
                slots = (0, 2) if a == AR else (0, 1, 2)
                for i in slots:
                    act.sem_inc(q["soft"][i], 1)
                with act.Fori(0, NG) as g:
                    for b in range(B):
                        for st in range(STEPS):
                            act.wait_ge(q["pv"][st % 2], 6 * g + 3 * b + st // 2 + 1)
                            for g4 in range(G if st < 5 else 1):
                                k = G * st + g4
                                if k % 3 not in slots:
                                    continue
                                lo = P * st if st < 4 else 0
                                act.wait_ge(q["unit"][k % 3], 14 * g + 7 * b + k // 3 + 1)
                                nc.scalar.activation(prob[:, st % 2, g4, lo:S], two(2 * (k % 3))[:, lo:S],
                                                     ACT.Relu if a == AR else ACT.Exp, scale=SCALE)\
                                    .then_inc(q["soft"][k % 3], 1)

            def reciprocal(i):
                for c in range(NC):
                    k = 4 * i + c
                    d = ch(dloc if i == R_LOC else dt_, c)
                    if i == R_LOC:
                        act.wait_ge(d_add, c + 1)
                        act.wait_ge(l_pv, B * KT)
                    elif i == R_AR:
                        act.wait_ge(d_add, 4 + c + 1)
                    else:
                        act.wait_ge(s_ol[c // CB], 32 * (i + 1))
                    nc.scalar.activation(rcp[:, 2, c], d, ACT.Ln).then_inc(d_ln, 1)
                    act.wait_ge(d_ln, k + 1)
                    nc.scalar.activation(rcp[:, 0, c], rcp[:, 2, c], ACT.Exp, scale=-1.0).then_inc(d_0, 1)

            def moe_layer(i):
                act.wait_ge(m_log, i + 1)
                nc.scalar.activation(rt[:, 0:16 * NE], bank(7)[:, 0:16 * NE], ACT.Exp, scale=-1.0)\
                    .then_inc(m_e, 1)
                for c in range(NC):
                    for j in range(NPAIR + 1):
                        k = (i * NC + c) * (NPAIR + 1) + j
                        r = P if j < NPAIR else INTER
                        act.wait_ge(m_gu, k + 1)
                        if k >= 2:
                            act.wait_ge(m_su, k - 1)
                        nc.scalar.activation(moe[0:r, 0, k % 2], ps[0:r, k % 2, :], ACT.Silu).then_inc(m_sg, 1)

            LOG_EXP = "natural_log_exp_and_others"
            nc.scalar.preload_act_table_set(LOG_EXP)
            act.wait_ge(s_cst, 48)
            act.wait_ge(s_set, 3)
            norm(0)
            parts_of(AW)
            band_soft(AW)
            reciprocal(R_AW)
            norm(1)
            norm(2)
            norm(3)
            parts_of(AG)
            full_soft(AG)
            reciprocal(R_AG)
            norm(4)
            parts_of(AL)
            band_soft(AL)
            reciprocal(R_AL)
            norm(5)
            norm(6)
            for c in range(NC):
                act.wait_ge(l_xt, c + 1)
                nc.scalar.activation(ch(xtr, c), bank(c), ACT.Identity, bias=v_("loc_b")).then_inc(l_xc, 1)
            for v in range(B * KT):
                act.wait_ge(l_w, v + 1)
                nc.scalar.activation(work[:, (2 + v % 2) * S:(3 + v % 2) * S], work[:, (v % 2) * S:(v % 2 + 1) * S],
                                     ACT.Tanh).then_inc(l_th, 1)
                act.wait_ge(l_th, v + 1)
                if v >= 2:
                    act.wait_ge(l_pv, v - 1)
                    act.wait_ge(l_acc, v - 1)
                nc.scalar.activation(work[:, (4 + v % 2) * S:(5 + v % 2) * S],
                                     work[:, (2 + v % 2) * S:(3 + v % 2) * S], ACT.Exp).then_inc(l_e, 1)
            nc.scalar.preload_act_table_set(LOG_EXP)
            reciprocal(R_LOC)
            norm(7)
            moe_layer(0)
            nc.scalar.preload_act_table_set(LOG_EXP)
            norm(8)
            norm(9)
            norm(10)
            parts_of(AR)
            full_soft(AR)
            reciprocal(R_AR)
            norm(11)
            for c in range(NC):
                for j in range(FF // P):
                    k = 4 * c + j
                    act.wait_ge(f_h, k + 1)
                    if c >= 2:
                        act.wait_ge(s_lin, outputs(U_FF, c - 2))
                    nc.scalar.activation(ffh[:, c % 2, j], bank(j), ACT.Relu,
                                         bias=v_(f"ff1_b{j}")).then_inc(f_r, 1)
            norm(12)
            moe_layer(1)

        @block.vector
        def _(dve):
            nc.vector.memzero(stf[:]).then_inc(s_set, 1)
            nc.vector.memset(eps[:, 0:1], 1e-5).then_inc(s_set, 1)
            nc.vector.memset(eps[:, 1:2], 1e-6).then_inc(s_set, 1)
            nc.vector.memset(vf[:, :, :, D:VW], 1.0).then_inc(s_set, 1)
            nc.vector.memzero(ps[:, 6:8, :]).then_inc(s_set, 1)

            def norm(n):
                src, dst, kind, g, b, _ = nrm(n)
                for c in range(NC):
                    i = 4 * n + c
                    dve.wait_ge(n_r, i + 1)
                    if kind == "rms":
                        nc.vector.scalar_tensor_tensor(out=ch(dst, c), in0=ch(src, c), scalar=v_(g), in1=nrr[:, c],
                                                       op0=ALU.mult, op1=ALU.mult).then_inc(n_z, 1)
                    elif g is None:
                        nc.vector.tensor_tensor(ch(dst, c), bank(c), nrr[:, c], ALU.mult).then_inc(n_z, 1)
                    else:
                        nc.vector.scalar_tensor_tensor(out=ch(dst, c), in0=bank(c), scalar=v_(g), in1=nrr[:, c],
                                                       op0=ALU.mult, op1=ALU.mult).then_inc(n_half, 1)
                        dve.wait_ge(n_half, 4 * (n - 9) + c + 1)
                        nc.vector.tensor_scalar(ch(dst, c), ch(dst, c), v_(b), None, ALU.add).then_inc(n_z, 1)

            def residual(u, dst, c, bias=None, src=None):
                dve.wait_ge(s_lin, outputs(u, c))
                last = u in (U_AL, U_FF)
                if bias is None:
                    ins = nc.vector.tensor_tensor(ch(dst, c), bank(4 + c), ch(dst, c), ALU.add)
                else:
                    ins = nc.vector.scalar_tensor_tensor(out=ch(dst, c), in0=bank(4 + c), scalar=v_(bias),
                                                         in1=ch(dst, c), op0=ALU.add, op1=ALU.add)
                if not last:
                    ins.then_inc(s_res, 1)
                    return
                ins.then_inc(s_mid, 1)
                dve.wait_ge(s_mid, (4 if u == U_FF else 0) + c + 1)
                nc.vector.tensor_tensor(ch(x, c), ch(x, c), ch(h, c), ALU.add).then_inc(s_res, 1)

            def project(a):
                nvh = KVH if GQA[a] else H
                for c in range(NC):
                    if ROPE[a]:
                        for t in range(2):
                            m = 2 * c + t
                            kr = 8 * a + m - 8
                            r = KVH * D if t else P
                            tab = ropek if t else ropeq
                            cols = slice((c % CB) * CH, (c % CB + 1) * CH)
                            rt_ = rope_t[0:r, m % 2]
                            dve.wait_ge(p_mm, 8 * a + m + 1)
                            if m == 0:
                                dve.wait_ge(s_rope, 32 * a)
                            if m >= 2:
                                dve.wait_ge(p_fn, kr - 1)
                            nc.vector.tensor_tensor(rt_[:, 0], ps[0:r, c, :], tab[:, 0, cols], ALU.mult)
                            nc.vector.tensor_tensor(rt_[:, 1], ps[0:r, 4 + c, :], tab[:, 1, cols], ALU.mult)\
                                .then_inc(p_t, 1)
                    dve.wait_ge(p_v, 4 * a + c + 1)
                    dst = vf[:, 4 * c:4 * c + 4, 0:nvh, 0:D]
                    src = bank(c)[:, 0:4 * nvh * D].rearrange("p (t h d) -> p t h d", t=4, d=D)
                    if a == AR:
                        bv = w_("r_bv").rearrange("p (h d) -> p h d", d=D)
                        for tt in range(4):
                            ins = nc.vector.tensor_tensor(dst[:, tt], src[:, tt], bv, ALU.add)
                    else:
                        ins = nc.vector.tensor_copy(dst, src)
                    ins.then_inc(p_vf, 1)

            def copy_out(a, g, b):
                q = A[a]
                dve.wait_ge(q["pv"][1], (2 * g + b + 2) if a in (AW, AL) else (6 * g + 3 * b + 4))
                dve.wait_ge(q["st"][b], 16 * g + 16)
                nc.vector.tensor_copy(oev[:, b, :], two(6)).then_inc(q["oev"][b], 1)

            def attention_loop(a):
                q = A[a]
                for b in range(B):
                    dve.sem_inc(q["oev"][b], 1)
                if a == AW:
                    for i in range(2):
                        dve.sem_inc(w_m[i], 1)
                if a == AR:
                    dve.sem_inc(q["soft"][1], 1)
                with dve.Fori(0, NG) as g:
                    if a == AW:
                        for b in range(B):
                            for k in range(16):
                                dve.wait_ge(w_s[k % 2], 16 * g + 8 * b + k // 2 + 1)
                                nc.vector.tensor_reduce(
                                    mxq[:, b, 2 * k:2 * k + 2],
                                    bank(4 + k % 2)[:, 0:2 * W_A].rearrange("p (t s) -> p t s", t=2),
                                    AX.X, ALU.max).then_inc(w_m[k % 2], 1)
                            n = 4 * (2 * g + b)
                            dve.wait_ge(w_t, 2 * g + b + 1)
                            nc.vector.tensor_scalar(mxt[:, b, 0], bank(4)[0:G * KT, 0:P], -1.0, None, ALU.mult)\
                                .then_inc(w_m[0], 1)
                            dve.wait_ge(w_m[0], 18 * g + 9 * b + 10)
                            nc.vector.tensor_copy(mxp[:, b, 0], mxt[:, b, 0]).then_inc(w_n, 1)
                            dve.wait_ge(w_n, n + 1)
                            nc.vector.tensor_tensor(mxt[:, b, 1], mxt[:, b, 0], mxp[:, b, 0], ALU.subtract)\
                                .then_inc(w_n, 1)
                            dve.wait_ge(w_n, n + 2)
                            nc.vector.tensor_copy(mxp[:, b, 1], mxt[:, b, 1]).then_inc(w_n, 1)
                            dve.wait_ge(w_n, n + 3)
                            nc.vector.tensor_tensor(mxp[:, b, 2], mxt[:, b, 1], mxp[:, b, 1], ALU.subtract)\
                                .then_inc(w_n, 1)
                    for b in range(B):
                        if a == AR:
                            for st in range(STEPS):
                                dve.wait_ge(q["pv"][st % 2], 6 * g + 3 * b + st // 2 + 1)
                                for g4 in range(G if st < 5 else 1):
                                    k = G * st + g4
                                    if k % 3 != 1:
                                        continue
                                    lo = P * st if st < 4 else 0
                                    dve.wait_ge(q["unit"][1], 14 * g + 7 * b + k // 3 + 1)
                                    nc.vector.tensor_scalar(prob[:, st % 2, g4, lo:S], two(2)[:, lo:S],
                                                            SCALE, 0.0, ALU.mult, ALU.max)\
                                        .then_inc(q["soft"][1], 1)
                        copy_out(a, g, b)

            def attention_end(a, u, dst, bias=None):
                i = RECIP_OF[a]
                for c in range(NC):
                    if a == AR:
                        dve.wait_ge(s_ol[c // CB], 32 * 4)
                        nc.vector.tensor_scalar(ch(dt_, c), ch(dt_, c), 1e-9, None, ALU.add).then_inc(d_add, 1)
                for c in range(NC):
                    k = 4 * i + c
                    dve.wait_ge(d_u, k + 1)
                    nc.vector.scalar_tensor_tensor(out=rcp[:, 2, c], in0=rcp[:, 1, c], scalar=-2.0,
                                                   in1=rcp[:, 0, c], op0=ALU.add, op1=ALU.mult).then_inc(d_v, 1)
                    dve.wait_ge(d_v, k + 1)
                    nc.vector.scalar_tensor_tensor(out=ch(ot, c), in0=ch(ot, c), scalar=-1.0,
                                                   in1=rcp[:, 2, c], op0=ALU.mult, op1=ALU.mult).then_inc(d_o, 1)
                for c in range(NC):
                    residual(u, dst, c, bias)

            def moe_layer(i):
                nt = T // P
                e, s_, sel, w8 = (rt[:, k * 256:(k + 1) * 256].rearrange("p (t e) -> p t e", t=nt) for k in range(4))
                bi = rt[:, 1024:1024 + nt * LANE].rearrange("p (t e) -> p t e", t=nt)
                rep = rt[:, 1344:1344 + nt * LANE].rearrange("p (t e) -> p t e", t=nt)
                top = rt[:, 1664:1664 + nt * 8].rearrange("p (t e) -> p t e", t=nt)
                tot = rt[:, 1792:1792 + nt]
                cw = rt[:, 0:256].rearrange("p (t e) -> p t e", t=nt)
                k0 = 12 * i
                step = [k0]

                def done(ins):
                    step[0] += 1
                    ins.then_inc(m_d, 1)

                def after():
                    dve.wait_ge(m_d, step[0])

                dve.wait_ge(m_e, i + 1)
                done(nc.vector.tensor_scalar(s_, e, 1.0, None, ALU.add))
                done(nc.vector.memset(bi[:, :, NE:LANE], NEG))
                after()
                done(nc.vector.reciprocal(s_, s_))
                after()
                done(nc.vector.tensor_tensor(bi[:, :, 0:NE], s_,
                                             w_("gate_b").unsqueeze(1).broadcast_to([P, nt, NE]), ALU.add))
                after()
                for t in range(nt):
                    ins = nc.vector.max(top[:, t], bi[:, t, 0:NE])
                done(ins)
                after()
                done(nc.vector.memset(top[:, :, TOPK:8], NEG))
                after()
                for t in range(nt):
                    ins = nc.vector.match_replace(rep[:, t], top[:, t], bi[:, t], 2 * NEG)
                done(ins)
                after()
                done(nc.vector.tensor_tensor(sel, rep[:, :, 0:NE], bi[:, :, 0:NE], ALU.not_equal))
                after()
                done(nc.vector.tensor_tensor(w8, s_, sel, ALU.mult))
                after()
                done(nc.vector.tensor_reduce(tot, w8, AX.X, ALU.add))
                after()
                done(nc.vector.reciprocal(tot, tot))
                after()
                done(nc.vector.scalar_tensor_tensor(out=cw, in0=w8, scalar=ROUTE,
                                                    in1=tot.unsqueeze(2).broadcast_to([P, nt, NE]),
                                                    op0=ALU.mult, op1=ALU.mult))
                assert step[0] == k0 + 12
                nc.vector.memzero(stf[:, 0:T // 2]).then_inc(m_cs, 1)
                for c in range(NC):
                    tmp = rt[0:NE, 512:1024]
                    p2 = stf[0:NE, T // 2:T // 2 + CH // 2].bitcast(BF16)
                    k = 4 * (4 * i + c)
                    dve.wait_ge(m_t, 4 * i + c + 1)
                    if c == 0:
                        dve.wait_ge(m_cs, 5 * i + 1)
                    nc.vector.tensor_copy(comb[0:NE, c * CH:(c + 1) * CH], bank(4 + c)[0:NE]).then_inc(m_c, 1)
                    dve.wait_ge(m_c, k + 1)
                    nc.vector.tensor_tensor(tmp, bank(4 + c)[0:NE], comb[0:NE, c * CH:(c + 1) * CH], ALU.subtract)\
                        .then_inc(m_c, 1)
                    dve.wait_ge(m_c, k + 2)
                    nc.vector.tensor_copy(p2, tmp).then_inc(m_c, 1)
                    dve.wait_ge(m_c, k + 3)
                    nc.vector.tensor_copy(comb[32:32 + NE, c * CH:(c + 1) * CH], p2).then_inc(m_c, 1)
                    nc.vector.tensor_tensor(comb[64:64 + NE, c * CH:(c + 1) * CH], tmp, p2, ALU.subtract)\
                        .then_inc(m_cs, 1)
                for c in range(NC):
                    for j in range(NPAIR + 1):
                        k = (i * NC + c) * (NPAIR + 1) + j
                        r = P if j < NPAIR else INTER
                        dve.wait_ge(m_sg, k + 1)
                        if k >= 2:
                            if j != 1:
                                dve.wait_ge(m_y, ((k - 2) // (NPAIR + 1)) * NPAIR + (k - 2) % (NPAIR + 1) + 1)
                            else:
                                dve.wait_ge(s_lin, outputs((U_M0, U_M1)[i], c - 1))
                        if j == NPAIR:
                            nc.vector.tensor_tensor(moe[0:r, 2, k % 2], ps[0:r, 2 + k % 2, :], moe[0:r, 0, k % 2],
                                                    ALU.mult).then_inc(m_su, 1)
                            continue
                        nc.vector.tensor_tensor(moe[:, 1, k % 2], bank(2 + k % 2), moe[:, 0, k % 2], ALU.mult)\
                            .then_inc(m_su, 1)
                        dve.wait_ge(m_su, k + 1)
                        nc.vector.tensor_tensor(moe[:, 2, k % 2], bank(4 + (c + 1 + k % 2) % 4), moe[:, 1, k % 2],
                                                ALU.mult).then_inc(m_h, 1)
                        if c and j == 1:
                            residual(U_M0 if i == 0 else U_M1, x, c - 1)
                residual(U_M0 if i == 0 else U_M1, x, NC - 1)

            for k in range(2):
                dve.wait_ge(s_fa, k + 1)
                nc.vector.tensor_copy(work[:, k * 128:(k + 1) * 128], ps[:, k, 0:128]).then_inc(s_fb, 1)
            dve.wait_ge(s_fa, 3)
            nc.vector.tensor_copy(fm[:], ps[:, 2, 0:128]).then_inc(s_fb, 1)
            dve.wait_ge(s_fa, 4)
            nc.vector.tensor_copy(g_kv[:], ps[:, 3, 0:96]).then_inc(s_fb, 1)
            dve.wait_ge(s_w, 32)
            dve.wait_ge(s_cst, 48)
            nc.vector.tensor_tensor(w_("sf_w"), w_("sf_w"), w_("sf_m"), ALU.mult).then_inc(s_fb, 1)

            norm(0)
            project(AW)
            attention_loop(AW)
            attention_end(AW, U_AW, x)
            norm(1)
            for c in range(NC):
                residual(U_F0, x, c, "f_b")
            norm(2)
            norm(3)
            project(AG)
            attention_loop(AG)
            attention_end(AG, U_AG, h)
            norm(4)
            project(AL)
            attention_loop(AL)
            attention_end(AL, U_AL, h)
            norm(5)
            for c in range(NC):
                residual(U_F1, x, c, "f_b")
            norm(6)
            for c in range(NC):
                dve.wait_ge(l_tr, c + 1)
                nc.vector.tensor_copy(zr[:, 4 * c:4 * c + 4, :].rearrange("p t d -> p (t d)"), bank(4 + c))\
                    .then_inc(l_tc, 1)
            near = c_("near")
            for v in range(B * KT + 1):
                if v < B * KT:
                    t = v % KT
                    dve.wait_ge(l_s, v + 1)
                    if v >= 2:
                        dve.wait_ge(l_th, v - 1)
                    nc.vector.tensor_tensor(work[:, (v % 2) * S:(v % 2 + 1) * S], two(2 * (v % 2)),
                                            near[:, P * (KT - 1 - t):P * (KT - 1 - t) + S], ALU.mult)\
                        .then_inc(l_w, 1)
                if v:
                    u = v - 1
                    b = u // KT
                    acc = dacc[:, b * S:(b + 1) * S]
                    wt = work[:, (4 + u % 2) * S:(5 + u % 2) * S]
                    dve.wait_ge(l_p, u + 1)
                    if u % KT == 0:
                        nc.vector.tensor_copy(acc, wt).then_inc(l_acc, 1)
                    else:
                        dve.wait_ge(l_acc, u)
                        nc.vector.tensor_tensor(acc, acc, wt, ALU.add).then_inc(l_acc, 1)
            for c in range(NC):
                dve.wait_ge(l_den, c + 1)
                nc.vector.tensor_scalar(ch(dloc, c), bank(c), 1e-7, None, ALU.add).then_inc(d_add, 1)
            for c in range(NC):
                k = 4 * R_LOC + c
                dve.wait_ge(d_u, k + 1)
                nc.vector.scalar_tensor_tensor(out=rcp[:, 2, c], in0=rcp[:, 1, c], scalar=-2.0,
                                               in1=rcp[:, 0, c], op0=ALU.add, op1=ALU.mult).then_inc(d_v, 1)
                dve.wait_ge(d_v, k + 1)
                dve.wait_ge(l_pv, B * KT)
                nc.vector.scalar_tensor_tensor(out=rcp[:, 2, c], in0=bank(4 + c), scalar=-1.0,
                                               in1=rcp[:, 2, c], op0=ALU.mult, op1=ALU.mult).then_inc(d_o, 1)
                dve.wait_ge(d_o, k + 1)
                nc.vector.tensor_tensor(ch(x, c), ch(x, c), rcp[:, 2, c], ALU.add).then_inc(s_res, 1)
            norm(7)
            moe_layer(0)
            norm(8)
            norm(9)
            for c in range(NC):
                residual(U_SF, h, c, "sf_b")
            norm(10)
            project(AR)
            attention_loop(AR)
            attention_end(AR, U_AR, h, "r_bo")
            norm(11)
            for c in range(NC):
                residual(U_FF, h, c, "ff2_b")
            norm(12)
            moe_layer(1)

        @block.tensor
        def _(pe):
            def mm(o, l, r, start=True, stop=True):
                return nc.tensor.matmul(o, l, r, start=start, stop=stop, skip_group_check=True)

            def norm(n):
                src, _, kind, _, _, _ = nrm(n)
                if kind == "ln":
                    for c in range(NC):
                        wait_source(pe, n, c)
                        mm(bank(c), c_("center"), ch(src, c)).then_inc(n_cen, 1)
                for c in range(NC):
                    pe.wait_ge(n_sq, 4 * n + c + 1)
                    mm(bank(4 + c), c_("mean"), nsq[:, c]).then_inc(n_var, 1)

            def project(a):
                n = N_OF[a]
                if a == AW:
                    wq, wk, wv = [(w_("a_wq"),)], [(w_("a_wk"),)], w_("a_wv")
                if a == AR:
                    wq, wk, wv = [(w_("r_wq"),)], [(w_("r_wk"),)], w_("r_wv")
                if a == AG:
                    wq, wk, wv = [(w_("g_wq"), w_("g_wqr"))], [(g_kv[:, 0:32], g_kv[:, 32:64])], g_kv[:, 64:96]
                if a == AL:
                    wq, wk, wv = [(w_("l_wq"), w_("l_wqr"))], [(w_("l_wk"), w_("l_wkr"))], w_("l_wv")
                r_v = KVH * D if GQA[a] else P
                for c in range(NC):
                    pe.wait_ge(n_z, 4 * n + c + 1)
                    for t in range(2):
                        m = 2 * c + t
                        k = 8 * a + m
                        ws = (wk if t else wq)[0]
                        if ROPE[a]:
                            r = KVH * D if t else P
                            kr = k - 8
                            if t:
                                pe.wait_ge(p_r, kr)
                            mm(ps[0:r, c, :], ws[0], ch(z, c))
                            mm(ps[0:r, 4 + c, :], ws[1], ch(z, c)).then_inc(p_mm, 1)
                            pe.wait_ge(p_sq, kr + 1)
                            rt_ = rope_t[0:r, m % 2]
                            mm(ps[0:r, c, :], c_("head_k", r) if t else c_("head_q"), rt_[:, 1]).then_inc(p_var, 1)
                        else:
                            mm(bank(c + 4 * t), ws[0], ch(z, c)).then_inc(p_mm, 1)
                    if ROPE[a]:
                        pe.wait_ge(p_r, 8 * a - 8 + 2 * c + 2)
                    else:
                        pe.wait_ge(p_f, (8 if a == AR else 0) + 2 * c + 1)
                    for tt in range(4):
                        ins = mm(bank(c)[:, tt * r_v:(tt + 1) * r_v],
                                 z[:, (4 * c + tt) * P:(4 * c + tt + 1) * P], wv)
                    ins.then_inc(p_v, 1)

            def start_loop(a):
                q = A[a]
                for s in q["pv"]:
                    pe.sem_inc(s, 1)
                pe.wait_ge(p_vf, 4 * (a + 1))
                pe.wait_ge(p_2, 8 * (a + 1))

            def band_loop(a):
                q = A[a]
                w = W_A if a == AW else W_L
                mask = b_("band_a") if a == AW else b_("band_l")
                start_loop(a)

                def maxima(g, b):
                    pe.wait_ge(q["stack"][b], 64 * (g + 1))
                    for k in range(16):
                        g4, j0 = k // 4, 2 * (k % 4)
                        pe.wait_ge(w_m[k % 2], (16 + 2 * (1 - k % 2)) * g + (8 + 1 - k % 2) * b + k // 2 + 1)
                        mm(bank(4 + k % 2)[:, 0:2 * W_A], b_("ident"), b_("band_q"), True, False)
                        for j in range(2):
                            t = j0 + j
                            ins = mm(bank(4 + k % 2)[:, j * W_A:(j + 1) * W_A], qst[:, b, g4, t * P:(t + 1) * P],
                                     kst[:, b, g4, t * P:t * P + W_A], False, j == 1)
                        ins.then_inc(w_s[k % 2], 1)
                    pe.wait_ge(w_m[0], 18 * g + 9 * b + 8 + 1)
                    pe.wait_ge(w_m[1], 16 * g + 8 * b + 8 + 1)
                    nc.tensor.transpose(bank(4)[0:G * KT, 0:P], mxq[:, b, :], c_("ident")).then_inc(w_t, 1)

                def scores(g, b, st):
                    for g4 in range(G):
                        k = G * st + g4
                        kg = 0 if GQA[a] else g4
                        pe.wait_ge(q["soft"][k % 2], 8 * g + 4 * b + k // 2 + 1)
                        for half in range(2):
                            o = bank(2 * (k % 2) + half)
                            mm(o[:, 0:2 * w], b_("ident"), mask, True, False)
                            for j in range(2):
                                t = 4 * st + 2 * half + j
                                wt = min(w, S - t * P)
                                ins = mm(o[:, j * w:j * w + wt], kst[:, b, kg, PAD + t * P:PAD + (t + 1) * P],
                                         qst[:, b, g4, t * P:t * P + wt], False, j == 1)
                        ins.then_inc(q["unit"][k % 2], 1)

                def values(g, b, st):
                    for g4 in range(G):
                        k = G * st + g4
                        pe.wait_ge(q["soft"][k % 2], 8 * g + 4 * b + k // 2 + 2)
                    if st == 0:
                        pe.wait_ge(q["vg"][b], g + 1)
                        pe.wait_ge(q["oev"][1 - b], g + 1 + b)
                    for j in range(4):
                        t = 4 * st + j
                        cuts = [(t * P, min(t * P + w, (t // 4 + 1) * CH))]
                        if t == 3:
                            cuts.append((CH, t * P + w))
                        for lo, hi in cuts:
                            for g4 in range(G):
                                kg = 0 if GQA[a] else g4
                                ins = mm(two(6)[32 * g4:32 * g4 + VW, lo:hi], vg[:, b, t, kg, :],
                                         prob[:, st, g4].rearrange("p (a s) -> p a s", a=2)
                                         [:, j // 2, (j % 2) * w + lo - t * P:(j % 2) * w + hi - t * P],
                                         lo in (0, CH) and t in (0, 3), t == KT - 1)
                    ins.then_inc(q["pv"][st], 1)

                with pe.Fori(0, NG) as g:
                    if a == AW:
                        maxima(g, 0)
                        maxima(g, 1)
                    for b in range(B):
                        if a == AW:
                            pe.wait_ge(w_l[b], 48 * (g + 1))
                        else:
                            pe.wait_ge(q["stack"][b], 32 * (g + 1))
                        scores(g, b, 0)
                        scores(g, b, 1)
                        values(g, b, 0)
                        values(g, b, 1)

            def full_loop(a):
                q = A[a]
                start_loop(a)

                def scores(g, b, st):
                    for g4 in range(G):
                        k = G * st + (g4 if st < 5 else 0)
                        kg = 0 if GQA[a] else g4
                        if st < 5 or g4 == 0:
                            pe.wait_ge(q["soft"][k % 3], 14 * g + 7 * b + k // 3 + 1)
                        o = two(2 * (k % 3))
                        for t, q0, lo, hi in reversed(pieces(st, g4)):
                            mm(o[:, lo:hi], kst[:, b, kg, PAD + t * P:PAD + (t + 1) * P],
                               qst[:, b, g4, q0:q0 + hi - lo], True, q0 != t * P)
                            if q0 == t * P:
                                ins = mm(o[:, lo:lo + P], b_("ident"), b_("causal"), False, True)
                        if st < 5 or g4 == G - 1:
                            ins.then_inc(q["unit"][k % 3], 1)

                def values(g, b, st):
                    for g4 in range(G if st < 5 else 1):
                        k = G * st + g4
                        pe.wait_ge(q["soft"][k % 3], 14 * g + 7 * b + k // 3 + 2)
                    if st == 0:
                        pe.wait_ge(q["vg"][b], g + 1)
                        pe.wait_ge(q["oev"][1 - b], g + 1 + b)
                    for n in range(len(pieces(st, 0))):
                        for g4 in range(G):
                            t, q0, lo, hi = pieces(st, g4)[n]
                            kg = 0 if GQA[a] else g4
                            pb = prob[:, st % 2, g4 if st < 5 else 0]
                            ins = mm(two(6)[32 * g4:32 * g4 + VW, q0:q0 + hi - lo], vg[:, b, t, kg, :],
                                     pb[:, lo:hi], t == 0, t == KT - 1)
                    ins.then_inc(q["pv"][st % 2], 1)

                with pe.Fori(0, NG) as g:
                    for b in range(B):
                        pe.wait_ge(q["stack"][b], 32 * (g + 1))
                        scores(g, b, 0)
                        for st in range(STEPS):
                            if st + 1 < STEPS:
                                scores(g, b, st + 1)
                            values(g, b, st)

            def attention_end(a, u, wo):
                i = RECIP_OF[a]
                for c in range(NC):
                    pe.wait_ge(d_o, 4 * i + c + 1)
                    mm(bank(4 + c), w_(wo), ch(ot, c)).then_inc(s_lin, 1)

            def linear(u, n, lhs):
                for c in range(NC):
                    pe.wait_ge(n_z, 4 * n + c + 1)
                    mm(bank(4 + c), lhs, ch(z, c)).then_inc(s_lin, 1)

            def moe_layer(i, n):
                pe.wait_ge(n_z, 4 * n + NC)
                for t in range(T // P):
                    ins = mm(bank(7)[:, t * NE:(t + 1) * NE], z[:, t * P:(t + 1) * P], w_("gate_w"))
                ins.then_inc(m_log, 1)
                cw = rt[:, 0:256].rearrange("p (t e) -> p t e", e=NE)
                pe.wait_ge(m_d, 12 * (i + 1))
                for c in range(NC):
                    for tt in range(4):
                        ins = nc.tensor.transpose(bank(4 + c)[0:NE, tt * P:(tt + 1) * P], cw[:, 4 * c + tt, :],
                                                  c_("ident"))
                    ins.then_inc(m_t, 1)
                pe.wait_ge(m_cs, 5 * (i + 1))

                def up(c, j):
                    k = (i * NC + c) * (NPAIR + 1) + j
                    r = P if j < NPAIR else INTER
                    if k >= 2:
                        pe.wait_ge(m_su, k - 1)
                    mm(ps[0:r, k % 2, :], w_("w_gate")[:, j * P:j * P + r], ch(z, c))
                    ins = mm(ps[0:r, 2 + k % 2, :], w_("w_up")[:, j * P:j * P + r], ch(z, c))
                    if j < NPAIR:
                        hid = (i * NC + c) * NPAIR + j
                        if hid - 1 > i * NC * NPAIR:
                            pe.wait_ge(m_h, hid - 1)
                        ins = mm(bank(4 + (c + 1 + k % 2) % 4), b_("spread")[:, j * P:(j + 1) * P],
                                 comb[:, c * CH:(c + 1) * CH])
                    ins.then_inc(m_gu, 1)

                def down(c, j):
                    k = (i * NC + c) * (NPAIR + 1) + j
                    r = P if j < NPAIR else INTER
                    if j < NPAIR:
                        pe.wait_ge(m_h, (i * NC + c) * NPAIR + j + 1)
                    else:
                        pe.wait_ge(m_su, k + 1)
                    return mm(bank(4 + c), w_("w_down", r)[:, j * P:j * P + P], moe[0:r, 2, k % 2], j == 0, j == NPAIR)

                todo = [(c, j) for c in range(NC) for j in range(NPAIR + 1)]
                up(*todo[0])
                for n_, (c, j) in enumerate(todo):
                    if n_ + 1 < len(todo):
                        up(*todo[n_ + 1])
                    ins = down(c, j)
                    if j < NPAIR:
                        ins.then_inc(m_y, 1)
                    else:
                        ins.then_inc(s_lin, 1)

            pe.wait_ge(s_cst, 48)
            pe.wait_ge(s_w, 32)
            mm(ps[:, 0, 0:128], w_("f_re"), c_("dft_c"), True, False)
            mm(ps[:, 0, 0:128], w_("f_im"), c_("dft_s"), False, True).then_inc(s_fa, 1)
            mm(ps[:, 1, 0:128], w_("f_im"), c_("dft_c"), True, False)
            mm(ps[:, 1, 0:128], w_("f_re"), c_("dft_ns"), False, True).then_inc(s_fa, 1)
            pe.wait_ge(s_fb, 2)
            mm(ps[:, 2, 0:128], work[:, 0:128], c_("idft_c"), True, False)
            mm(ps[:, 2, 0:128], work[:, 128:256], c_("idft_ns"), False, True).then_inc(s_fa, 1)
            a0 = WAT["g_kup"][0]
            mm(ps[:, 3, 0:96], w_("g_kvd", 32), wsb[0:32, a0:a0 + 96]).then_inc(s_fa, 1)
            pe.wait_ge(s_fb, 5)
            pe.wait_ge(s_set, 5)

            norm(0)
            project(AW)
            band_loop(AW)
            attention_end(AW, U_AW, "a_wo")
            norm(1)
            linear(U_F0, 1, fm[:])
            norm(2)
            norm(3)
            project(AG)
            full_loop(AG)
            attention_end(AG, U_AG, "g_wo")
            norm(4)
            project(AL)
            band_loop(AL)
            attention_end(AL, U_AL, "l_wo")
            norm(5)
            linear(U_F1, 5, fm[:])
            norm(6)
            for c in range(NC):
                pe.wait_ge(n_z, 4 * 6 + c + 1)
                mm(bank(c), w_("loc_w"), ch(z, c)).then_inc(l_xt, 1)
                for tt in range(4):
                    t = 4 * c + tt
                    ins = nc.tensor.transpose(bank(4 + c)[:, tt * P:(tt + 1) * P], z[:, t * P:(t + 1) * P],
                                              c_("ident"))
                ins.then_inc(l_tr, 1)
            pe.wait_ge(l_xc, NC)
            pe.wait_ge(l_tc, NC)
            for v in range(B * KT + 1):
                if v < B * KT:
                    b = v // KT
                    if v >= 2:
                        pe.wait_ge(l_w, v - 1)
                    for half in range(2):
                        ins = mm(bank(2 * (v % 2) + half), z[:, v * P:(v + 1) * P], ch(xtr, CB * b + half))
                    ins.then_inc(l_s, 1)
                if v:
                    u = v - 1
                    b = u // KT
                    pe.wait_ge(l_p, u + 1)
                    for half in range(2):
                        ins = mm(bank(4 + CB * b + half), zr[:, u, :],
                                 work[:, (4 + u % 2) * S + half * CH:(4 + u % 2) * S + (half + 1) * CH],
                                 u % KT == 0, u % KT == KT - 1)
                    ins.then_inc(l_pv, 1)
            for c in range(NC):
                if c == 0:
                    pe.wait_ge(l_acc, B * KT)
                    pe.wait_ge(l_w, B * KT)
                mm(bank(c), c_("ones"), ch(dacc, c)).then_inc(l_den, 1)
            norm(7)
            moe_layer(0, 7)
            norm(8)
            norm(9)
            linear(U_SF, 9, w_("sf_w"))
            norm(10)
            project(AR)
            full_loop(AR)
            attention_end(AR, U_AR, "r_wo")
            norm(11)
            for c in range(NC):
                pe.wait_ge(n_z, 4 * 11 + c + 1)
                for j in range(FF // P):
                    if c:
                        pe.wait_ge(f_r, 4 * (c - 1) + j + 1)
                    elif j:
                        pe.wait_ge(n_z, 4 * 11 + j + 1)
                    mm(bank(j), w_("ff1")[:, j * P:(j + 1) * P], ch(z, c)).then_inc(f_h, 1)
                for j in range(FF // P):
                    pe.wait_ge(f_r, 4 * c + j + 1)
                    ins = mm(bank(4 + c), w_("ff2")[:, j * P:(j + 1) * P], ffh[:, c % 2, j], j == 0, j == 3)
                ins.then_inc(s_lin, 1)
            norm(12)
            moe_layer(1, 12)



def bf16_parts(v):
    out, rest = [], v.astype(np.float32)
    for _ in range(3):
        part = rest.astype(BF16_NP)
        out.append(part)
        rest = rest - part.astype(np.float32)
    return out


def float_constants():
    c = np.zeros((P, CN), np.float32)

    def put(name, v):
        a, b = CAT[name]
        c[0:v.shape[0], a:b] = v

    i = np.arange(P)
    ang = 2.0 * np.pi * ((i[:, None] * i[None, :]) % P) / P
    put("dft_c", np.cos(ang))
    put("dft_s", np.sin(ang))
    put("dft_ns", -np.sin(ang))
    put("idft_c", np.cos(ang) / P)
    put("idft_ns", -np.sin(ang) / P)
    put("ident", np.eye(P))
    put("center", np.eye(P) - 1.0 / P)
    put("mean", np.full((P, P), 1.0 / P))
    put("ones", np.ones((P, P)))
    put("head_q", (i[:, None] % H == i[None, :] % H) / D)
    j = np.arange(KVH * D)
    put("head_k", (j[:, None] % KVH == j[None, :] % KVH) / D)
    put("offdiag", 1.0 - np.eye(P))
    dist = np.abs(np.arange(P * (2 * KT - 1))[None, :] - P * (KT - 1) - i[:, None]).astype(np.float32)
    near = np.float32(1.0) / (dist + np.float32(1e-7)) * (dist != 0).astype(np.float32)
    put("near", near)
    return c


def bfloat_constants():
    c = np.zeros((P, BN), np.float32)

    def put(name, v):
        a, b = BAT[name]
        c[0:v.shape[0], a:b] = v

    i = np.arange(P)[:, None]
    put("ident", np.eye(P))
    w = np.arange(W_A)[None, :]
    ok = (i - w + PAD >= 0) & (i - w + PAD <= WIN_A)
    put("band_q", np.tile(np.where(ok, 0.0, NEG), (1, 2)))
    ok = (w - i >= 0) & (w - i <= WIN_A)
    put("band_a", np.tile(np.where(ok, 0.0, NEG), (1, 2)))
    w = np.arange(W_L)[None, :]
    ok = (w - i >= 0) & (w - i < WIN_L)
    put("band_l", np.tile(np.where(ok, 0.0, NEG), (1, 2)))
    put("causal", np.where(np.arange(P)[None, :] >= i, 0.0, NEG))
    spread = np.zeros((P, NPAIR, 2, INTER), np.float32)
    for e in range(NE):
        for part in range(3):
            spread[32 * part + e, e // 2, e % 2, :] = 1.0
    put("spread", spread.reshape(P, -1))
    return c.astype(BF16_NP)


def rope_tables():
    q = np.zeros((2, 2, P, S), np.float32)
    k = np.zeros((2, 2, KVH * D, S), np.float32)
    for n, base in enumerate((1000000.0, 10000.0)):
        inv = np.float32(1.0) / np.float32(base) ** (np.arange(0, D, 2, dtype=np.float32) / np.float32(D))
        f = np.arange(S, dtype=np.float32)[:, None] * inv.astype(np.float32)[None, :]
        cos, sin = np.cos(f).astype(np.float32), np.sin(f).astype(np.float32)
        for d in range(D):
            sg = -1.0 if d % 2 == 0 else 1.0
            q[n, 0, d * H:(d + 1) * H] = cos[:, d // 2]
            q[n, 1, d * H:(d + 1) * H] = sg * sin[:, d // 2]
            k[n, 0, d * KVH:(d + 1) * KVH] = cos[:, d // 2]
            k[n, 1, d * KVH:(d + 1) * KVH] = sg * sin[:, d // 2]
    return q, k


def window_bias():
    slope = np.exp2(-(np.arange(H, dtype=np.float32) + 1.0) * 8.0 / H).astype(np.float32)
    c = bf16_parts(slope * np.sqrt(np.float32(D)))
    q = np.zeros((XROWS, H, S), np.float32)
    k = np.zeros((XROWS, H, SL), np.float32)
    t = np.arange(S)
    lo, odd = t % P, (t // P) % 2
    for i in range(3):
        ci = c[i].astype(np.float32)[:, None]
        q[i], k[i, :, PAD:] = lo[None], ci
        q[3 + i], k[3 + i, :, PAD:] = ci, -lo[None]
        q[6 + i], k[6 + i, :, PAD:] = P * odd[None], ci * (1 - odd)[None]
        q[9 + i], k[9 + i, :, PAD:] = P * (1 - odd)[None], ci * odd[None]
    q[12] = 1.0
    k[12, :, 0:PAD] = NEG
    k[13:16, :, PAD:] = 1.0
    return q.astype(BF16_NP), k.astype(BF16_NP)



def kernel(**inputs):
    import concourse.bacc as _bacc
    from concourse.bass_utils import run_bass_kernel_spmd as _run

    v = {k: np.ascontiguousarray(a) for k, a in inputs.items()}
    pq = np.array([hd * D + d for d in range(D) for hd in range(H)])
    pqr = np.array([hd * D + (d ^ 1) for d in range(D) for hd in range(H)])
    pk = np.array([hd * D + d for d in range(D) for hd in range(KVH)])
    pkr = np.array([hd * D + (d ^ 1) for d in range(D) for hd in range(KVH)])

    w = np.zeros((P, WN), np.float32)

    def put(name, a):
        lo, hi = WAT[name]
        w[0:a.shape[0], lo:hi] = a

    w_in = v["L0_attn_a_w_in"].T
    put("a_wq", w_in[:, 0:E][:, pq])
    put("a_wk", w_in[:, E:2 * E][:, pq])
    put("a_wv", w_in[:, 2 * E:])
    put("a_wo", v["L0_attn_a_w_out"].T)
    put("g_wq", v["L0_attn_b_g_wq"][:, pq])
    put("g_wqr", v["L0_attn_b_g_wq"][:, pqr])
    put("g_wo", v["L0_attn_b_g_wo"])
    put("g_kvd", v["L0_attn_b_g_kv_down"].T)
    put("g_kup", v["L0_attn_b_g_k_up"][:, pk])
    put("g_kupr", v["L0_attn_b_g_k_up"][:, pkr])
    put("g_vup", v["L0_attn_b_g_v_up"])
    put("l_wq", v["L0_attn_b_l_wq"][:, pq])
    put("l_wqr", v["L0_attn_b_l_wq"][:, pqr])
    put("l_wk", v["L0_attn_b_l_wk"][:, pk])
    put("l_wkr", v["L0_attn_b_l_wk"][:, pkr])
    put("l_wv", v["L0_attn_b_l_wv"])
    put("l_wo", v["L0_attn_b_l_wo"])
    put("f_re", v["L0_ffn_w_freq_real"])
    put("f_im", v["L0_ffn_w_freq_imag"])
    put("loc_w", v["L1_attn_a_W"])
    put("sf_w", v["L1_attn_b_sf_w"].T)
    put("sf_m", v["L1_attn_b_mask"].T)
    put("r_wq", v["L1_attn_b_wq"].T[:, pq])
    put("r_wk", v["L1_attn_b_wk"].T[:, pq])
    put("r_wv", v["L1_attn_b_wv"].T)
    put("r_wo", v["L1_attn_b_wo"].T)
    put("r_bv", np.broadcast_to(v["L1_attn_b_bv"][None, :], (P, E)))
    put("ff1", v["L1_attn_b_ff1_w"].T)
    put("ff2", v["L1_attn_b_ff2_w"].T.reshape(FF // P, P, E).transpose(1, 0, 2).reshape(P, FF))
    put("gate_w", v["L1_ffn_gate_w"].T)
    put("gate_b", np.broadcast_to(v["L1_ffn_gate_b"][None, :], (P, NE)))
    w13 = v["L1_ffn_w13"].transpose(2, 0, 1)
    put("w_gate", np.concatenate([w13[:, :, 0:INTER].reshape(P, -1), v["L1_ffn_w13_s"].T[:, 0:INTER]], axis=1))
    put("w_up", np.concatenate([w13[:, :, INTER:].reshape(P, -1), v["L1_ffn_w13_s"].T[:, INTER:]], axis=1))
    lo, hi = WAT["w_down"]
    w[:, lo:hi - P] = v["L1_ffn_w2"].transpose(0, 2, 1).reshape(NPAIR, P, E).transpose(1, 0, 2).reshape(P, -1)
    w[0:INTER, hi - P:hi] = v["L1_ffn_w2_s"].T
    vec = np.zeros((P, len(VCOLS)), np.float32)
    names = {"n1": "L0_attn_b_norm1_w", "n2": "L0_attn_b_norm2_w", "f_b": "L0_ffn_bias", "loc_b": "L1_attn_a_b",
             "sf_b": "L1_attn_b_sf_b", "r_bo": "L1_attn_b_bo", "ff2_b": "L1_attn_b_ff2_b"}
    names.update({n: f"L1_attn_b_{n}" for n in ("g1", "b1", "g2", "b2", "g3", "b3")})
    for n, full in names.items():
        vec[:, VAT[n]] = v[full]
    vec[:, VAT["r_bq"]] = v["L1_attn_b_bq"][pq]
    vec[:, VAT["r_bk"]] = v["L1_attn_b_bk"][pq]
    for j in range(FF // P):
        vec[:, VAT[f"ff1_b{j}"]] = v["L1_attn_b_ff1_b"][j * P:(j + 1) * P]

    rq, rk = rope_tables()
    bq, bk = window_bias()
    arrays = {
        "in_x": np.ascontiguousarray(v["L0_attn_a_x"].reshape(T, E).T), "in_w": w, "in_v": vec,
        "in_c": float_constants(), "in_b": bfloat_constants(), "in_rq": rq, "in_rk": rk, "in_bq": bq, "in_bk": bk,
    }
    nc = _bacc.Bacc("TRN2", target_bir_lowering=False, num_devices=1)
    args = [nc.dram_tensor(n, a.shape, mybir.dt.from_np(a.dtype), kind="ExternalInput").ap()
            for n, a in arrays.items()]
    args.append(nc.dram_tensor("out_x", (E, T), F32, kind="ExternalOutput").ap())
    build(nc, *args)
    r = _run(nc, [arrays], core_ids=[0])
    return np.ascontiguousarray(r.results[0]["out_x"].T).reshape(B, S, E)
```

```python
from contextlib import ExitStack

import numpy as np

import concourse.bass as bass
from concourse import mybir

F32 = mybir.dt.float32
BF16 = mybir.dt.bfloat16
BF16_NP = mybir.dt.np(BF16)
ALU = mybir.AluOpType
ACT = mybir.ActivationFunctionType
AX = mybir.AxisListType

B, S, E = 2, 1024, 128
T = B * S
CH = 512
NC = T // CH
CB = S // CH
P = 128
H, D = 16, E // 16
KVH = 4
G = 4
NG = H // G
KT = S // P
VW = 2 * D
ROWS = 9 * D
PAD = 64
SL = S + PAD
XROWS = 16
WIN_A, WIN_L = 64, 32
W_A, W_L = P + WIN_A, P + WIN_L
NEG = -1e30
SCALE = float(1.0 / np.sqrt(np.float32(D)))
NE, INTER, TOPK = 16, 64, 4
ROUTE = 2.5
NPAIR = NE // 2
FF = 4 * E
LANE = 20

AW, AG, AL, AR = 0, 1, 2, 3
GQA = (False, True, True, False)
ROPE = (False, True, True, False)
U_AW, U_F0, U_AG, U_AL, U_F1, U_LOC, U_M0, U_SF, U_AR, U_FF, U_M1 = range(11)
R_AW, R_AG, R_AL, R_LOC, R_AR = range(5)
RECIP_OF = {AW: R_AW, AG: R_AG, AL: R_AL, AR: R_AR}

WCOLS = [
    ("a_wq", 128), ("a_wk", 128), ("a_wv", 128), ("a_wo", 128),
    ("g_wq", 128), ("g_wqr", 128), ("g_wo", 128), ("g_kvd", 128), ("g_kup", 32), ("g_kupr", 32), ("g_vup", 32),
    ("l_wq", 128), ("l_wqr", 128), ("l_wk", 32), ("l_wkr", 32), ("l_wv", 32), ("l_wo", 128),
    ("f_re", 128), ("f_im", 128), ("loc_w", 128),
    ("sf_w", 128), ("sf_m", 128), ("r_wq", 128), ("r_wk", 128), ("r_wv", 128), ("r_wo", 128), ("r_bv", 128),
    ("ff1", FF), ("ff2", FF), ("gate_w", NE), ("gate_b", NE),
    ("w_gate", NPAIR * 128 + INTER), ("w_up", NPAIR * 128 + INTER), ("w_down", NPAIR * 128 + 128),
]
VCOLS = ["n1", "n2", "f_b", "loc_b", "sf_b", "r_bq", "r_bk", "r_bo", "ff1_b0", "ff1_b1", "ff1_b2", "ff1_b3",
         "ff2_b", "g1", "b1", "g2", "b2", "g3", "b3"]
CCOLS = [("dft_c", 128), ("dft_s", 128), ("dft_ns", 128), ("idft_c", 128), ("idft_ns", 128), ("ident", 128),
         ("center", 128), ("mean", 128), ("ones", 128), ("head_q", 128), ("head_k", 32), ("offdiag", 128),
         ("near", P * (2 * KT - 1))]
BCOLS = [("ident", 128), ("band_q", 2 * W_A), ("band_a", 2 * W_A), ("band_l", 2 * W_L), ("causal", 128),
         ("spread", NPAIR * 128)]


def columns(spec):
    at, out = 0, {}
    for name, n in spec:
        out[name] = (at, at + n)
        at += n
    return out, at


WAT, WN = columns(WCOLS)
CAT, CN = columns(CCOLS)
BAT, BN = columns(BCOLS)
VAT = {name: i for i, name in enumerate(VCOLS)}


def build(nc, xt, wp, vp, cp, bp, rope_q, rope_k, bias_q, bias_k, out):
    ctx = ExitStack()
    with ctx:
        def sb(name, shape, dt):
            return ctx.enter_context(nc.sbuf_tensor(name, shape, dt))

        def sem(name):
            return ctx.enter_context(nc.semaphore(name))

        x = sb("x", [P, T], F32)
        h = sb("h", [P, T], F32)
        z = sb("z", [P, T], F32)
        wsb = sb("wsb", [P, WN], F32)
        vsb = sb("vsb", [P, len(VCOLS)], F32)
        csb = sb("csb", [P, CN], F32)
        bsb = sb("bsb", [P, BN], BF16)
        eps = sb("eps", [P, 2], F32)
        fm = sb("fm", [P, 128], F32)
        g_kv = sb("g_kv", [P, 96], F32)
        ropeq = sb("ropeq", [P, 2, S], F32)
        ropek = sb("ropek", [KVH * D, 2, S], F32)
        nsq = sb("nsq", [P, NC, CH], F32)
        nrr = sb("nrr", [P, NC, CH], F32)
        vf = sb("vf", [P, B * KT, H, VW], F32)
        aux = sb("aux", [P, 6 * CH], F32)
        mxq = sb("mxq", [P, B, G * KT], F32)
        mxt = sb("mxt", [G * KT, B, 2, P], F32)
        mxp = sb("mxp", [G * KT, B, 3, P], BF16)
        stf = sb("stf", [P, B * G * (S + SL) // 2], F32)
        work = sb("work", [P, 16 * CH], F32)
        qst = stf[:, 0:B * G * S // 2].bitcast(BF16).rearrange("p (b g s) -> p b g s", b=B, g=G)
        kst = stf[:, B * G * S // 2:].bitcast(BF16).rearrange("p (b g s) -> p b g s", b=B, g=G)
        oev = aux[:, 0:4 * CH].rearrange("p (b s) -> p b s", b=B)
        vg = aux[:, 4 * CH:6 * CH].rearrange("p (b t g v) -> p b t g v", b=B, t=KT, g=G)
        prob = work[:].rearrange("p (s g w) -> p s g w", s=2, g=G)
        wbf = work[:, 0:12 * CH].bitcast(BF16).rearrange("p (t b i s) -> p t b i s", t=2, b=B, i=3)
        qf = work[:, 12 * CH:14 * CH].rearrange("p (m s) -> p m s", m=2)
        rem = work[:, 14 * CH:16 * CH].rearrange("p (m s) -> p m s", m=2)
        rope_t = aux[:].rearrange("p (m k s) -> p m k s", m=2, k=3)
        ot = nsq[:].rearrange("p c s -> p (c s)")
        dt_ = nrr[:].rearrange("p c s -> p (c s)")
        rcp = work[:, 0:12 * CH].rearrange("p (k c s) -> p k c s", k=3, c=NC)
        xtr = stf[:, 0:T]
        zr = stf[:, T:2 * T].rearrange("p (t d) -> p t d", t=B * KT)
        dacc = stf[:, 2 * T:3 * T]
        dloc = stf[:, 3 * T:4 * T]
        comb = stf[:, 0:T // 2].bitcast(BF16)
        moe = work[:, 0:12 * CH].rearrange("p (k m s) -> p k m s", k=6, m=2)
        rt = stf[:, T:T + 2048]
        cparts = stf[:, 2 * T:2 * T + 768].bitcast(BF16).rearrange("p (t i e) -> p t i e", i=3, e=32)
        shared = work[:, 12 * CH:14 * CH].rearrange("p (m s) -> p m s", m=2)
        ffh = work[:, 0:8 * CH].rearrange("p (m k s) -> p m k s", m=2, k=4)

        ps = ctx.enter_context(nc.psum_tensor("ps", [P, 8, CH], F32))

        def bank(i):
            return ps[:, i, :]

        def two(i):
            return ps[:, i:i + 2, :].rearrange("p a s -> p (a s)")

        def w_(name, rows=P):
            a, b = WAT[name]
            return wsb[0:rows, a:b]

        def c_(name, rows=P):
            a, b = CAT[name]
            return csb[0:rows, a:b]

        def b_(name):
            a, b = BAT[name]
            return bsb[:, a:b]

        def v_(name, rows=P):
            return vsb[0:rows, VAT[name]:VAT[name] + 1]

        def ch(t, c):
            return t[:, c * CH:(c + 1) * CH]

        scr_q = nc.dram_tensor("scr_q", (B, NG, 3, D, G * S), BF16, kind="Internal").ap()
        scr_k = nc.dram_tensor("scr_k", (B, NG, 3, D, G * SL), BF16, kind="Internal").ap()
        scr_kg = nc.dram_tensor("scr_kg", (B, KVH, 3, D, SL), BF16, kind="Internal").ap()
        scr_o = nc.dram_tensor("scr_o", (NG, P, T), F32, kind="Internal").ap()

        s_x = sem("x_loaded")
        s_nc = sem("norm_constants_loaded")
        s_w0 = sem("first_weights_loaded")
        s_w = sem("weights_loaded")
        s_cst = sem("constants_loaded")
        s_rope = sem("rope_loaded")
        s_set = sem("memory_set")
        s_zero = sem("stack_rows_zeroed")
        s_fa = sem("fourier_a")
        s_fb = sem("fourier_b")
        n_cen = sem("norm_centered")
        n_sq = sem("norm_squared")
        n_var = sem("norm_variance")
        n_ln = sem("norm_log")
        n_r = sem("norm_factor")
        n_half = sem("norm_scaled")
        n_z = sem("norm_done")
        s_lin = sem("layer_out")
        s_res = sem("residual_done")
        s_mid = sem("residual_mid")
        p_mm = sem("proj_in_psum")
        p_t = sem("rope_products")
        p_rot = sem("rope_sum")
        p_sq = sem("head_squares")
        p_var = sem("head_variance")
        p_ln = sem("head_log")
        p_r = sem("head_factor")
        p_f = sem("proj_float")
        p_fn = sem("proj_normed")
        p_1 = sem("part_1")
        p_r1 = sem("rest_1")
        p_2 = sem("part_2")
        p_3 = sem("part_3")
        p_v = sem("values_in_psum")
        p_vf = sem("values_copied")
        s_pad = sem("key_padding_stored")
        s_scr = [sem(f"parts_stored{b}") for b in range(B)]
        s_ol = [sem(f"attention_out_loaded{b}") for b in range(B)]
        s_dl = [sem(f"denominator_loaded{b}") for b in range(B)]
        d_add = sem("denominator_guarded")
        d_ln = sem("denominator_log")
        d_0 = sem("reciprocal_guess")
        d_u = sem("reciprocal_product")
        d_v = sem("reciprocal_done")
        d_o = sem("attention_normed")
        l_xt = sem("loc_transformed")
        l_xc = sem("loc_transformed_copied")
        l_tr = sem("loc_transposed")
        l_tc = sem("loc_transposed_copied")
        l_s = sem("loc_scores")
        l_w = sem("loc_weighted")
        l_th = sem("loc_tanh")
        l_e = sem("loc_exp")
        l_p = sem("loc_diagonal_cleared")
        l_acc = sem("loc_sum")
        l_pv = sem("loc_values")
        l_den = sem("loc_denominator")
        m_log = sem("route_logits")
        m_e = sem("route_exp")
        m_d = sem("route_step")
        m_t = sem("route_transposed")
        m_z = sem("route_room_zeroed")
        m_cs = sem("route_stack")
        e_gu = sem("shared_gate_up")
        e_a = sem("shared_silu_and_up")
        e_m = sem("shared_hidden")
        e_y = sem("shared_down")
        e_o = sem("shared_copied")
        e_x = sem("shared_added")
        m_gu = sem("expert_gate_up")
        m_sg = sem("expert_silu")
        m_su = sem("expert_product")
        m_h = sem("expert_hidden")
        m_y = sem("expert_down")
        f_h = sem("ff_hidden_in_psum")
        f_r = sem("ff_hidden")
        s_out = sem("out_stored")

        A = []
        for a, tag in enumerate(("win", "glob", "loc", "relu")):
            A.append(dict(
                stack=[sem(f"{tag}_stack_loaded{b}") for b in range(B)],
                vg=[sem(f"{tag}_values_ready{b}") for b in range(B)],
                unit=[sem(f"{tag}_unit{i}") for i in range(3)],
                soft=[sem(f"{tag}_probs{i}") for i in range(3)],
                pv=[sem(f"{tag}_pv{i}") for i in range(2)],
                oev=[sem(f"{tag}_out_copied{b}") for b in range(B)],
                st=[sem(f"{tag}_out_stored{b}") for b in range(B)],
            ))
        w_s = [sem(f"max_scores{i}") for i in range(2)]
        w_m = [sem(f"max_taken{i}") for i in range(2)]
        w_t = sem("max_transposed")
        w_n = sem("max_step")
        w_l = [sem(f"max_rows_loaded{b}") for b in range(B)]

        block = ctx.enter_context(nc.Block())

        def nrm(n):
            return [
                (x, z, "ln", None, None, (s_x, None)),
                (x, z, "ln", None, None, (s_res, U_AW)),
                (x, h, "ln", None, None, (s_res, U_F0)),
                (h, z, "rms", "n1", None, (n_z, 2)),
                (h, z, "rms", "n2", None, (s_res, U_AG)),
                (x, z, "ln", None, None, (s_res, U_AL)),
                (x, z, "ln", None, None, (s_res, U_F1)),
                (x, z, "ln", None, None, (s_res, U_LOC)),
                (x, h, "ln", None, None, (s_res, U_M0)),
                (h, z, "ln", "g1", "b1", (n_z, 8)),
                (h, z, "ln", "g2", "b2", (s_res, U_SF)),
                (h, z, "ln", "g3", "b3", (s_res, U_AR)),
                (x, z, "ln", None, None, (s_res, U_FF)),
            ][n]

        N_OF = {AW: 0, AG: 3, AL: 4, AR: 10}

        def wait_source(eng, n, c):
            s, k = nrm(n)[5]
            eng.wait_ge(s, 16 * NC if k is None else 4 * k + c + 1)

        def outputs(u, c):
            return 4 * (u - (u > U_LOC)) + c + 1

        def spread_bank(c, j):
            return 4 + (c + 1 + (c + j) % 2) % 4

        ROUTE_STEPS = 16

        def pieces(step, g):
            if step < 4:
                return [(step, P * step, P * step, CH), (step, CH, CH, S)]
            if step == 4:
                return [(5, 5 * P, 0, 3 * P), (7, 7 * P, 3 * P, 4 * P), (4, 4 * P, CH, S)]
            return [(6, 6 * P, 2 * P * g, 2 * P * g + 2 * P)]

        LAG = (1, 2, 2, 1)
        MAX_AFTER = (2, 2, 2, 2, 2, 2, 2, 2)
        STEPS = 6

        @block.sync
        def _(sp):
            for c in range(NC):
                sp.dma_start(ch(x, c), xt[:, c * CH:(c + 1) * CH]).then_inc(s_x, 16)
            n_first = CAT["ones"][0]
            w_first = WAT["a_wo"][0]
            sp.dma_start(csb[:, 0:n_first], cp[:, 0:n_first]).then_inc(s_nc, 16)
            sp.dma_start(wsb[:, 0:w_first], wp[:, 0:w_first]).then_inc(s_w0, 16)
            sp.dma_start(bsb[:], bp).then_inc(s_cst, 16)
            sp.dma_start(vsb[:], vp).then_inc(s_cst, 16)
            sp.dma_start(csb[:, n_first:CN], cp[:, n_first:CN]).then_inc(s_cst, 16)
            sp.dma_start(wsb[:, w_first:WN], wp[:, w_first:WN]).then_inc(s_w, 16)

            def rope_load(i):
                sp.dma_start(ropeq[:], rope_q[i].rearrange("k p s -> p k s")).then_inc(s_rope, 16)
                sp.dma_start(ropek[:], rope_k[i].rearrange("k p s -> p k s")).then_inc(s_rope, 16)

            def store_parts(a, b):
                for i in range(3):
                    for t in range(2):
                        rows = KVH * D if t and GQA[a] else P
                        dst = scr_q if t == 0 else (scr_kg if GQA[a] else scr_k)
                        done = 8 * a + 2 * (CB * b + CB - 1) + t + 1
                        sp.wait_ge([p_1, p_2, p_3][i], done)
                        if dst is scr_kg:
                            to = dst[b, :, i].rearrange("g d s -> d g s")[:, :, PAD:SL]
                        else:
                            to = dst[b, :, i].rearrange("g d (h s) -> g (d h) s", h=G)
                            if t:
                                to = to[:, :, PAD:SL]
                        sp.dma_start(to, wbf[0:rows, t, b, i]).then_inc(s_scr[b], 16)
                sp.wait_ge(s_scr[b], 16 * 6 * (a + 1))

            def load_q(a, g, b):
                q = A[a]
                parts = scr_q[b, bass.ds(g, 1)].rearrange("g i d s -> (g i) d s")
                for i in range(3):
                    sp.dma_start(qst[3 * D * i:3 * D * (i + 1), b].rearrange("p h s -> p (h s)"),
                                 parts[i:i + 1].broadcast_to([3, D, G * S])).then_inc(q["stack"][b], 16)
                if a == AW:
                    sp.dma_start(qst[ROWS:ROWS + XROWS, b], bias_q[:, bass.ds(G * g, G), :])\
                      .then_inc(q["stack"][b], 16)

            def load_k(a, g, b):
                q = A[a]
                nh = 1 if GQA[a] else G
                parts = (scr_kg if GQA[a] else scr_k)[b, bass.ds(g, 1)].rearrange("g j d s -> g (j d) s")
                sp.dma_start(kst[0:ROWS, b, 0:nh, :].rearrange("p h s -> p (h s)"),
                             parts.broadcast_to([3, 3 * D, nh * SL])).then_inc(q["stack"][b], 16)
                if a == AW:
                    sp.dma_start(kst[ROWS:ROWS + XROWS, b], bias_k[:, bass.ds(G * g, G), :])\
                      .then_inc(q["stack"][b], 16)

            def load_max(g, b):
                sp.wait_ge(w_n, 4 * (2 * g + b + 1))
                for i in range(3):
                    r = ROWS + XROWS - 3 + i
                    sp.dma_start(qst[r:r + 1, b].rearrange("p g s -> p (g s)"), mxp[:, b, i, :]).then_inc(w_l[b], 16)

            def store_out(a, g, b, last):
                q = A[a]
                sp.wait_ge(q["oev"][b], g + 2)
                if last:
                    for k, t in ((1, dt_), (0, ot)):
                        for g4 in range(G):
                            to = D * (G * g + g4)
                            sp.dma_start(t[to:to + D, b * S:(b + 1) * S],
                                         oev[32 * g4 + k * D:32 * g4 + (k + 1) * D, b, :])\
                              .then_inc((s_ol if k == 0 else s_dl)[b], 16)
                    return
                sp.dma_start(scr_o[bass.ds(g, 1), :, b * S:(b + 1) * S].rearrange("g p s -> (g p) s"),
                             oev[:, b, :]).then_inc(q["st"][b], 16)

            def attention(a):
                q = A[a]
                for b in range(B):
                    sp.sem_inc(q["st"][b], 16)
                if a != AW:
                    sp.wait_ge(s_zero, a + 1)
                for b in range(B):
                    store_parts(a, b)
                    load_q(a, 0, b)
                    load_k(a, 0, b)

                if a == AW:
                    load_max(0, 0)

                def body(g, last):
                    for b in range(B):
                        if not last:
                            if a in (AW, AL):
                                sp.wait_ge(q["unit"][1], 8 * g + 4 * b + 4)
                            else:
                                sp.wait_ge(q["unit"][2], 14 * g + 7 * b + 7)
                            load_q(a, g + 1, b)
                            load_k(a, g + 1, b)
                        if a == AW and not (last and b == B - 1):
                            load_max(g + (b + 1) // B, (b + 1) % B)
                        store_out(a, g, b, last)

                with sp.Fori(0, NG - 1) as g:
                    body(g, False)
                for b in range(B):
                    sp.wait_ge(q["st"][b], 16 * NG)
                    for k, t in ((1, dt_), (0, ot)):
                        src = scr_o[0:NG - 1].rearrange("g (q r) s -> (g q) r s", q=G)
                        sp.dma_start(t[0:G * D * (NG - 1), b * S:(b + 1) * S],
                                     src[:, k * D:(k + 1) * D, b * S:(b + 1) * S])\
                          .then_inc((s_ol if k == 0 else s_dl)[b], 16)
                body(NG - 1, True)

            sp.wait_ge(s_zero, 1)
            zeros = stf[0:B * NG * 3 * D // 2, 0:G * PAD].bitcast(BF16)
            sp.dma_start(scr_k.rearrange("b g i d (h s) -> (b g i d h) s", h=G)[:, 0:PAD], zeros).then_inc(s_pad, 16)
            sp.dma_start(scr_kg.rearrange("b g i d s -> (b g i d) s")[:, 0:PAD],
                         zeros[:, 0:2 * PAD]).then_inc(s_pad, 16)
            sp.wait_ge(s_pad, 32)
            attention(AW)
            rope_load(0)
            attention(AG)
            sp.wait_ge(p_t, 8)
            rope_load(1)
            attention(AL)
            attention(AR)
            for c in range(NC):
                sp.wait_ge(s_res, 4 * U_M1 + c + 1)
                sp.dma_start(out[:, c * CH:(c + 1) * CH], ch(x, c)).then_inc(s_out, 16)
            sp.wait_ge(s_out, 16 * NC)

        @block.gpsimd
        def _(pool):
            def rest_of(a):
                def third(m):
                    k = 8 * a + m
                    c, t = m // 2, m % 2
                    r = KVH * D if t and GQA[a] else P
                    pool.wait_ge(p_2, k + 1)
                    part = wbf[0:r, t, c // CB, :, (c % CB) * CH:(c % CB + 1) * CH]
                    nc.gpsimd.tensor_tensor(part[:, 2], rem[0:r, t], part[:, 1], ALU.subtract).then_inc(p_3, 1)

                for m in range(2 * NC + LAG[a]):
                    if ROPE[a] and m < 2 * NC:
                        k, kr, t = 8 * a + m, 8 * a + m - 8, m % 2
                        r = KVH * D if t else P
                        pool.wait_ge(p_r, kr + 1)
                        if m >= 2:
                            pool.wait_ge(p_1, k - 1)
                            pool.wait_ge(p_r1, k - 1)
                        nc.gpsimd.tensor_tensor(qf[0:r, t], rope_t[0:r, t, 0], rope_t[0:r, t, 2], ALU.mult)\
                            .then_inc(p_fn, 1)
                    if m >= LAG[a]:
                        third(m - LAG[a])

            def group_values(a):
                q = A[a]
                pool.wait_ge(p_vf, 4 * (a + 1))
                pool.wait_ge(p_3, 8 * (a + 1))
                nvh, nh = (1, 1) if GQA[a] else (G, G)
                with pool.Fori(0, NG) as g:
                    for b in range(B):
                        pool.wait_ge(q["oev"][b], g + 1)
                        nc.gpsimd.tensor_copy(vg[:, b, :, 0:nh, :],
                                              vf[:, b * KT:(b + 1) * KT, bass.ds(nvh * g, nvh), :])\
                            .then_inc(q["vg"][b], 1)

            def reciprocal(i):
                for c in range(NC):
                    d = ch(dloc if i == R_LOC else dt_, c)
                    pool.wait_ge(d_0, 4 * i + c + 1)
                    nc.gpsimd.tensor_tensor(rcp[:, 1, c], d, rcp[:, 0, c], ALU.mult).then_inc(d_u, 1)

            def attention(a):
                if a != AW:
                    pool.wait_ge(s_res, 4 * {AG: U_AW, AL: U_AG, AR: U_M0}[a] + 4)
                    nc.gpsimd.memset(stf[64:P, :], 0.0).then_inc(s_zero, 1)
                    pool.wait_ge(s_zero, a + 1)
                rest_of(a)
                group_values(a)
                reciprocal(RECIP_OF[a])

            def moe_layer(i):
                pool.wait_ge(s_res, 4 * (U_LOC, U_AR)[i] + 4)
                nc.gpsimd.memset(cparts, 0.0).then_inc(m_z, 1)
                pool.wait_ge(m_z, 2 * i + 1)
                nc.gpsimd.memset(comb[96:P, :], 0.0).then_inc(m_z, 1)
                pool.wait_ge(m_z, 2 * i + 2)
                for c in range(NC + 1):
                    k = NC * i + c
                    if c < NC:
                        pool.wait_ge(e_a, k + 1)
                        if c >= 2:
                            pool.wait_ge(e_y, k - 1)
                            pool.wait_ge(e_x, k - 1)
                        nc.gpsimd.tensor_tensor(moe[0:INTER, 5, c % 2], moe[0:INTER, 3, c % 2],
                                                moe[0:INTER, 4, c % 2], ALU.mult).then_inc(e_m, 1)
                    if c:
                        pool.wait_ge(e_m, min(k + 1, NC * i + NC))
                        pool.wait_ge(e_o, k)
                        nc.gpsimd.tensor_tensor(ch(x, c - 1), ch(x, c - 1), shared[:, (c - 1) % 2], ALU.add)\
                            .then_inc(e_x, 1)

            nc.gpsimd.memset(stf[:], 0.0).then_inc(s_zero, 1)
            pool.wait_ge(s_zero, 1)
            attention(AW)
            attention(AG)
            attention(AL)
            pool.wait_ge(s_cst, 48)
            for v in range(B * KT):
                t = v % KT
                blk = work[:, (4 + v % 2) * S + t * P:(4 + v % 2) * S + (t + 1) * P]
                pool.wait_ge(l_e, v + 1)
                nc.gpsimd.tensor_tensor(blk, blk, c_("offdiag"), ALU.mult).then_inc(l_p, 1)
            reciprocal(R_LOC)
            moe_layer(0)
            attention(AR)
            moe_layer(1)

        @block.scalar
        def _(act):
            def norm(n):
                src, _, kind, _, _, _ = nrm(n)
                for c in range(NC):
                    i = 4 * n + c
                    if kind == "ln":
                        act.wait_ge(n_cen, i + 1 - 4 * (n > 3) - 4 * (n > 4))
                        nc.scalar.activation(nsq[:, c], bank(c), ACT.Square).then_inc(n_sq, 1)
                    else:
                        wait_source(act, n, c)
                        nc.scalar.activation(nsq[:, c], ch(src, c), ACT.Square).then_inc(n_sq, 1)
                e = eps[:, 0:1] if kind == "ln" else eps[:, 1:2]
                for c in range(NC):
                    i = 4 * n + c
                    act.wait_ge(n_var, i + 1)
                    nc.scalar.activation(nrr[:, c], bank(4 + c), ACT.Ln, bias=e).then_inc(n_ln, 1)
                    act.wait_ge(n_ln, i + 1)
                    nc.scalar.activation(nrr[:, c], nrr[:, c], ACT.Exp, scale=-0.5).then_inc(n_r, 1)

            def parts_of(a):
                def part(m, n):
                    c, t = m // 2, m % 2
                    r = KVH * D if t and GQA[a] else P
                    return wbf[0:r, t, c // CB, n, (c % CB) * CH:(c % CB + 1) * CH]

                def first(m):
                    t = m % 2
                    r = KVH * D if t and GQA[a] else P
                    if ROPE[a]:
                        act.wait_ge(p_fn, 8 * (a - 1) + m + 1)
                    else:
                        act.wait_ge(p_f, (8 if a == AR else 0) + m + 1)
                    nc.scalar.activation(part(m, 0), qf[0:r, t], ACT.Copy).then_inc(p_1, 1)

                def second(m):
                    t = m % 2
                    r = KVH * D if t and GQA[a] else P
                    act.wait_ge(p_r1, 8 * a + m + 1)
                    nc.scalar.activation(part(m, 1), rem[0:r, t], ACT.Copy).then_inc(p_2, 1)

                for m in range(2 * NC + LAG[a]):
                    if not ROPE[a]:
                        if m < 2 * NC:
                            first(m)
                        if m:
                            second(m - 1)
                        continue
                    kr, t = 8 * a + m - 8, m % 2
                    r = KVH * D if t else P
                    if m < 2 * NC:
                        rt_ = rope_t[0:r, t]
                        act.wait_ge(p_rot, kr + 1)
                        nc.scalar.activation(rt_[:, 1], rt_[:, 0], ACT.Square).then_inc(p_sq, 1)
                    if 1 <= m <= 2 * NC:
                        first(m - 1)
                    if m < 2 * NC:
                        act.wait_ge(p_var, kr + 1)
                        nc.scalar.activation(rt_[:, 2], ps[0:r, 2 * (m % 3), :], ACT.Ln, bias=eps[0:r, 1:2])\
                            .then_inc(p_ln, 1)
                        act.wait_ge(p_ln, kr + 1)
                        nc.scalar.activation(rt_[:, 2], rt_[:, 2], ACT.Exp, scale=-0.5).then_inc(p_r, 1)
                    if m >= LAG[a]:
                        second(m - LAG[a])

            def parts_are_stored(a):
                for b in range(B):
                    act.wait_ge(s_scr[b], 16 * 6 * (a + 1))

            def band_soft(a):
                q = A[a]
                w = W_A if a == AW else W_L
                parts_are_stored(a)
                for i in range(2):
                    act.sem_inc(q["soft"][i], 1)
                with act.Fori(0, NG) as g:
                    for b in range(B):
                        for st in range(2):
                            act.wait_ge(q["pv"][st], 2 * g + b + 1)
                            for g4 in range(G):
                                k = G * st + g4
                                act.wait_ge(q["unit"][k % 2], 8 * g + 4 * b + k // 2 + 1)
                                src = ps[:, 2 * (k % 2):2 * (k % 2) + 2, 0:2 * w]
                                dst = prob[:, st, g4].rearrange("p (a s) -> p a s", a=2)[:, :, 0:2 * w]
                                nc.scalar.activation(dst, src, ACT.Exp, scale=SCALE).then_inc(q["soft"][k % 2], 1)

            def full_soft(a):
                q = A[a]
                slots = (0, 2) if a == AR else (0, 1, 2)
                parts_are_stored(a)
                for i in slots:
                    act.sem_inc(q["soft"][i], 1)
                with act.Fori(0, NG) as g:
                    for b in range(B):
                        for st in range(STEPS):
                            act.wait_ge(q["pv"][st % 2], 6 * g + 3 * b + st // 2 + 1)
                            for g4 in range(G if st < 5 else 1):
                                k = G * st + g4
                                if k % 3 not in slots:
                                    continue
                                lo = P * st if st < 4 else 0
                                act.wait_ge(q["unit"][k % 3], 14 * g + 7 * b + k // 3 + 1)
                                nc.scalar.activation(prob[:, st % 2, g4, lo:S], two(2 * (k % 3))[:, lo:S],
                                                     ACT.Relu if a == AR else ACT.Exp, scale=SCALE)\
                                    .then_inc(q["soft"][k % 3], 1)

            def reciprocal(i):
                if i != R_LOC:
                    a = {r: a for a, r in RECIP_OF.items()}[i]
                    act.wait_ge(A[a]["pv"][1], (2 if a in (AW, AL) else 6) * NG + 1)
                for c in range(NC):
                    k = 4 * i + c
                    d = ch(dloc if i == R_LOC else dt_, c)
                    if i == R_LOC:
                        act.wait_ge(d_add, c + 1)
                        act.wait_ge(l_pv, B * KT)
                    elif i == R_AR:
                        act.wait_ge(d_add, 4 + c + 1)
                    else:
                        act.wait_ge(s_dl[c // CB], 80 * (i + 1))
                    nc.scalar.activation(rcp[:, 2, c], d, ACT.Ln).then_inc(d_ln, 1)
                    act.wait_ge(d_ln, k + 1)
                    nc.scalar.activation(rcp[:, 0, c], rcp[:, 2, c], ACT.Exp, scale=-1.0).then_inc(d_0, 1)

            def moe_layer(i):
                act.wait_ge(m_log, i + 1)
                nc.scalar.activation(rt[:, 0:16 * NE], bank(7)[:, 0:16 * NE], ACT.Exp, scale=-1.0)\
                    .then_inc(m_e, 1)
                for c in range(NC + 1):
                    k = NC * i + c
                    if c < NC:
                        act.wait_ge(e_gu, k + 1)
                        if c >= 2:
                            act.wait_ge(e_m, k - 1)
                        nc.scalar.activation(moe[0:INTER, 3, c % 2], ps[0:INTER, c % 2, :], ACT.Silu)
                        nc.scalar.activation(moe[0:INTER, 4, c % 2], ps[0:INTER, 2 + c % 2, :], ACT.Copy)\
                            .then_inc(e_a, 1)
                    if c:
                        act.wait_ge(e_y, k)
                        if c > 2:
                            act.wait_ge(e_x, k - 2)
                        nc.scalar.activation(shared[:, (c - 1) % 2], bank(4 + c - 1), ACT.Copy).then_inc(e_o, 1)
                for c in range(NC):
                    act.wait_ge(m_t, NC * i + c + 1)
                    nc.scalar.activation(comb[0:96, c * CH:(c + 1) * CH], bank(4 + c)[0:96], ACT.Copy)\
                        .then_inc(m_cs, 1)
                for c in range(NC):
                    for j in range(NPAIR):
                        k = (i * NC + c) * NPAIR + j
                        act.wait_ge(m_gu, k + 1)
                        if k >= 2:
                            act.wait_ge(m_su, k - 1)
                        nc.scalar.activation(moe[:, 0, k % 2], bank(k % 2), ACT.Silu).then_inc(m_sg, 1)

            LOG_EXP = "natural_log_exp_and_others"
            nc.scalar.preload_act_table_set(LOG_EXP)
            act.wait_ge(s_set, 2)
            norm(0)
            parts_of(AW)
            act.wait_ge(s_cst, 48)
            band_soft(AW)
            reciprocal(R_AW)
            norm(1)
            norm(2)
            norm(3)
            parts_of(AG)
            full_soft(AG)
            reciprocal(R_AG)
            norm(4)
            parts_of(AL)
            band_soft(AL)
            reciprocal(R_AL)
            norm(5)
            norm(6)
            for c in range(NC):
                act.wait_ge(l_xt, c + 1)
                nc.scalar.activation(ch(xtr, c), bank(c), ACT.Identity, bias=v_("loc_b")).then_inc(l_xc, 1)
            for v in range(B * KT):
                act.wait_ge(l_w, v + 1)
                nc.scalar.activation(work[:, (2 + v % 2) * S:(3 + v % 2) * S], work[:, (v % 2) * S:(v % 2 + 1) * S],
                                     ACT.Tanh).then_inc(l_th, 1)
                act.wait_ge(l_th, v + 1)
                if v >= 2:
                    act.wait_ge(l_pv, v - 1)
                    act.wait_ge(l_acc, v - 1)
                nc.scalar.activation(work[:, (4 + v % 2) * S:(5 + v % 2) * S],
                                     work[:, (2 + v % 2) * S:(3 + v % 2) * S], ACT.Exp).then_inc(l_e, 1)
            nc.scalar.preload_act_table_set(LOG_EXP)
            reciprocal(R_LOC)
            norm(7)
            moe_layer(0)
            nc.scalar.preload_act_table_set(LOG_EXP)
            norm(8)
            norm(9)
            norm(10)
            parts_of(AR)
            full_soft(AR)
            reciprocal(R_AR)
            norm(11)
            for c in range(NC):
                for j in range(FF // P):
                    k = 4 * c + j
                    act.wait_ge(f_h, k + 1)
                    if c >= 2:
                        act.wait_ge(s_lin, outputs(U_FF, c - 2))
                    nc.scalar.activation(ffh[:, c % 2, j], bank(j), ACT.Relu,
                                         bias=v_(f"ff1_b{j}")).then_inc(f_r, 1)
            norm(12)
            moe_layer(1)

        @block.vector
        def _(dve):
            nc.vector.memset(eps[:, 0:1], 1e-5).then_inc(s_set, 1)
            nc.vector.memset(eps[:, 1:2], 1e-6).then_inc(s_set, 1)
            nc.vector.memset(vf[:, :, :, D:VW], 1.0).then_inc(s_set, 1)
            nc.vector.memzero(ps[:, 6:8, :]).then_inc(s_set, 1)

            def norm(n):
                src, dst, kind, g, b, _ = nrm(n)
                for c in range(NC):
                    i = 4 * n + c
                    dve.wait_ge(n_r, i + 1)
                    if kind == "rms":
                        nc.vector.scalar_tensor_tensor(out=ch(dst, c), in0=ch(src, c), scalar=v_(g), in1=nrr[:, c],
                                                       op0=ALU.mult, op1=ALU.mult).then_inc(n_z, 1)
                    elif g is None:
                        nc.vector.tensor_tensor(ch(dst, c), bank(c), nrr[:, c], ALU.mult).then_inc(n_z, 1)
                    else:
                        nc.vector.scalar_tensor_tensor(out=ch(dst, c), in0=bank(c), scalar=v_(g), in1=nrr[:, c],
                                                       op0=ALU.mult, op1=ALU.mult).then_inc(n_half, 1)
                        dve.wait_ge(n_half, 4 * (n - 9) + c + 1)
                        nc.vector.tensor_scalar(ch(dst, c), ch(dst, c), v_(b), None, ALU.add).then_inc(n_z, 1)

            def residual(u, dst, c, bias=None, src=None):
                dve.wait_ge(s_lin, outputs(u, c))
                last = u in (U_AL, U_FF)
                if bias is None:
                    ins = nc.vector.tensor_tensor(ch(dst, c), bank(4 + c), ch(dst, c), ALU.add)
                else:
                    ins = nc.vector.scalar_tensor_tensor(out=ch(dst, c), in0=bank(4 + c), scalar=v_(bias),
                                                         in1=ch(dst, c), op0=ALU.add, op1=ALU.add)
                if not last:
                    ins.then_inc(s_res, 1)
                    return
                ins.then_inc(s_mid, 1)
                dve.wait_ge(s_mid, (4 if u == U_FF else 0) + c + 1)
                nc.vector.tensor_tensor(ch(x, c), ch(x, c), ch(h, c), ALU.add).then_inc(s_res, 1)

            def project(a):
                nvh = KVH if GQA[a] else H

                def rotary(m):
                    k, kr, c, t = 8 * a + m, 8 * a + m - 8, m // 2, m % 2
                    r = KVH * D if t else P
                    tab = ropek if t else ropeq
                    cols = slice((c % CB) * CH, (c % CB + 1) * CH)
                    rt_ = rope_t[0:r, t]
                    dve.wait_ge(p_mm, k + 1)
                    if m == 0:
                        dve.wait_ge(s_rope, 32 * a)
                    if m >= 2:
                        dve.wait_ge(p_fn, kr - 1)
                    nc.vector.tensor_tensor(rt_[:, 0], ps[0:r, 2 * (m % 3), :], tab[:, 0, cols], ALU.mult)
                    nc.vector.tensor_tensor(rt_[:, 1], ps[0:r, 2 * (m % 3) + 1, :], tab[:, 1, cols], ALU.mult)\
                        .then_inc(p_t, 1)
                    dve.wait_ge(p_t, kr + 1)
                    nc.vector.tensor_tensor(rt_[:, 0], rt_[:, 0], rt_[:, 1], ALU.add).then_inc(p_rot, 1)

                def float_copy(m):
                    c, t = m // 2, m % 2
                    dve.wait_ge(p_mm, 8 * a + m + 1)
                    if m >= 2:
                        dve.wait_ge(p_r1, 8 * a + m - 1)
                    if a == AR:
                        ins = nc.vector.tensor_scalar(qf[:, t], bank(c + 4 * t), v_("r_bk" if t else "r_bq"), None,
                                                      ALU.add)
                    else:
                        ins = nc.vector.tensor_copy(qf[:, t], bank(c + 4 * t))
                    ins.then_inc(p_f, 1)

                def rest(m):
                    k, c, t = 8 * a + m, m // 2, m % 2
                    r = KVH * D if t and GQA[a] else P
                    if not ROPE[a]:
                        dve.wait_ge(p_f, (8 if a == AR else 0) + m + 1)
                    dve.wait_ge(p_1, k + 1)
                    if m >= 2:
                        dve.wait_ge(p_2, k - 1)
                        dve.wait_ge(p_3, k - 1)
                    part = wbf[0:r, t, c // CB, 0, (c % CB) * CH:(c % CB + 1) * CH]
                    nc.vector.tensor_tensor(rem[0:r, t], qf[0:r, t], part, ALU.subtract).then_inc(p_r1, 1)

                def copy_values(c):
                    dve.wait_ge(p_v, 4 * a + c + 1)
                    dst = vf[:, 4 * c:4 * c + 4, 0:nvh, 0:D]
                    src = bank(6 + c % 2 if ROPE[a] else c)[:, 0:4 * nvh * D]\
                        .rearrange("p (t h d) -> p t h d", t=4, d=D)
                    if a == AR:
                        bv = w_("r_bv").rearrange("p (h d) -> p h d", d=D)
                        for tt in range(4):
                            ins = nc.vector.tensor_tensor(dst[:, tt], src[:, tt], bv, ALU.add)
                    else:
                        ins = nc.vector.tensor_copy(dst, src)
                    ins.then_inc(p_vf, 1)

                for m in range(2 * NC + LAG[a]):
                    if m < 2 * NC:
                        rotary(m) if ROPE[a] else float_copy(m)
                    if m >= LAG[a]:
                        rest(m - LAG[a])
                    if m and m % 2 == 0:
                        copy_values(m // 2 - 1)

            def copy_out(a, g, b):
                q = A[a]
                dve.wait_ge(q["pv"][1], (2 * g + b + 2) if a in (AW, AL) else (6 * g + 3 * b + 4))
                dve.wait_ge(q["st"][b], 16 * g + 16)
                nc.vector.tensor_copy(oev[:, b, :], two(6)).then_inc(q["oev"][b], 1)

            def attention_loop(a):
                q = A[a]
                for b in range(B):
                    dve.sem_inc(q["oev"][b], 1)
                if a == AW:
                    for i in range(2):
                        dve.sem_inc(w_m[i], 1)
                if a == AR:
                    dve.sem_inc(q["soft"][1], 1)

                def maxima(g, b):
                    for k in range(16):
                        dve.wait_ge(w_s[k % 2], 16 * g + 8 * b + k // 2 + 1)
                        nc.vector.tensor_reduce(
                            mxq[:, b, 2 * k:2 * k + 2],
                            bank(4 + k % 2)[:, 0:2 * W_A].rearrange("p (t s) -> p t s", t=2),
                            AX.X, ALU.max).then_inc(w_m[k % 2], 1)
                    n = 4 * (2 * g + b)
                    dve.wait_ge(w_t, 2 * g + b + 1)
                    nc.vector.tensor_scalar(mxt[:, b, 0], bank(4)[0:G * KT, 0:P], -1.0, None, ALU.mult)\
                        .then_inc(w_m[0], 1)
                    dve.wait_ge(w_m[0], 18 * g + 9 * b + 10)
                    nc.vector.tensor_copy(mxp[:, b, 0], mxt[:, b, 0]).then_inc(w_n, 1)
                    dve.wait_ge(w_n, n + 1)
                    nc.vector.tensor_tensor(mxt[:, b, 1], mxt[:, b, 0], mxp[:, b, 0], ALU.subtract)\
                        .then_inc(w_n, 1)
                    dve.wait_ge(w_n, n + 2)
                    nc.vector.tensor_copy(mxp[:, b, 1], mxt[:, b, 1]).then_inc(w_n, 1)
                    dve.wait_ge(w_n, n + 3)
                    nc.vector.tensor_tensor(mxp[:, b, 2], mxt[:, b, 1], mxp[:, b, 1], ALU.subtract)\
                        .then_inc(w_n, 1)

                def relu_units(g, b):
                    for st in range(STEPS):
                        dve.wait_ge(q["pv"][st % 2], 6 * g + 3 * b + st // 2 + 1)
                        for g4 in range(G if st < 5 else 1):
                            k = G * st + g4
                            if k % 3 != 1:
                                continue
                            lo = P * st if st < 4 else 0
                            dve.wait_ge(q["unit"][1], 14 * g + 7 * b + k // 3 + 1)
                            nc.vector.tensor_scalar(prob[:, st % 2, g4, lo:S], two(2)[:, lo:S],
                                                    SCALE, 0.0, ALU.mult, ALU.max)\
                                .then_inc(q["soft"][1], 1)

                def body(g, last):
                    for b in range(B):
                        if a == AW and not (last and b == B - 1):
                            maxima(g + (b + 1) // B, (b + 1) % B)
                        if a == AR:
                            relu_units(g, b)
                        copy_out(a, g, b)

                if a == AW:
                    maxima(0, 0)
                    with dve.Fori(0, NG - 1) as g:
                        body(g, False)
                    body(NG - 1, True)
                else:
                    with dve.Fori(0, NG) as g:
                        body(g, False)

            def attention_end(a, u, dst, bias=None):
                i = RECIP_OF[a]
                for c in range(NC):
                    if a == AR:
                        dve.wait_ge(s_dl[c // CB], 80 * (AR + 1))
                        nc.vector.tensor_scalar(ch(dt_, c), ch(dt_, c), 1e-9, None, ALU.add).then_inc(d_add, 1)
                for c in range(NC):
                    k = 4 * i + c
                    dve.wait_ge(d_u, k + 1)
                    nc.vector.scalar_tensor_tensor(out=rcp[:, 2, c], in0=rcp[:, 1, c], scalar=-2.0,
                                                   in1=rcp[:, 0, c], op0=ALU.add, op1=ALU.mult).then_inc(d_v, 1)
                    dve.wait_ge(d_v, k + 1)
                    dve.wait_ge(s_ol[c // CB], 80 * (a + 1))
                    nc.vector.scalar_tensor_tensor(out=ch(ot, c), in0=ch(ot, c), scalar=-1.0,
                                                   in1=rcp[:, 2, c], op0=ALU.mult, op1=ALU.mult).then_inc(d_o, 1)
                for c in range(NC):
                    residual(u, dst, c, bias)

            def moe_layer(i):
                nt = T // P
                e, s_, sel, w8 = (rt[:, k * 256:(k + 1) * 256].rearrange("p (t e) -> p t e", t=nt) for k in range(4))
                bi = rt[:, 1024:1024 + nt * LANE].rearrange("p (t e) -> p t e", t=nt)
                rep = rt[:, 1344:1344 + nt * LANE].rearrange("p (t e) -> p t e", t=nt)
                top = rt[:, 1664:1664 + nt * 8].rearrange("p (t e) -> p t e", t=nt)
                tot = rt[:, 1792:1792 + nt]
                cw = rt[:, 0:256].rearrange("p (t e) -> p t e", t=nt)
                k0 = ROUTE_STEPS * i
                step = [k0]

                def done(ins):
                    step[0] += 1
                    ins.then_inc(m_d, 1)

                def after():
                    dve.wait_ge(m_d, step[0])

                dve.wait_ge(m_e, i + 1)
                done(nc.vector.tensor_scalar(s_, e, 1.0, None, ALU.add))
                done(nc.vector.memset(bi[:, :, NE:LANE], NEG))
                after()
                done(nc.vector.reciprocal(s_, s_))
                after()
                done(nc.vector.tensor_tensor(bi[:, :, 0:NE], s_,
                                             w_("gate_b").unsqueeze(1).broadcast_to([P, nt, NE]), ALU.add))
                after()
                for t in range(nt):
                    ins = nc.vector.max(top[:, t], bi[:, t, 0:NE])
                done(ins)
                after()
                done(nc.vector.memset(top[:, :, TOPK:8], NEG))
                after()
                for t in range(nt):
                    ins = nc.vector.match_replace(rep[:, t], top[:, t], bi[:, t], 2 * NEG)
                done(ins)
                after()
                done(nc.vector.tensor_tensor(sel, rep[:, :, 0:NE], bi[:, :, 0:NE], ALU.not_equal))
                after()
                done(nc.vector.tensor_tensor(w8, s_, sel, ALU.mult))
                after()
                done(nc.vector.tensor_reduce(tot, w8, AX.X, ALU.add))
                after()
                done(nc.vector.reciprocal(tot, tot))
                after()
                dve.wait_ge(m_z, 2 * (i + 1))
                done(nc.vector.scalar_tensor_tensor(out=cw, in0=w8, scalar=ROUTE,
                                                    in1=tot.unsqueeze(2).broadcast_to([P, nt, NE]),
                                                    op0=ALU.mult, op1=ALU.mult))
                rest = s_
                after()
                done(nc.vector.tensor_copy(cparts[:, :, 0, 0:NE], cw))
                after()
                done(nc.vector.tensor_tensor(rest, cw, cparts[:, :, 0, 0:NE], ALU.subtract))
                after()
                done(nc.vector.tensor_copy(cparts[:, :, 1, 0:NE], rest))
                after()
                done(nc.vector.tensor_tensor(cparts[:, :, 2, 0:NE], rest, cparts[:, :, 1, 0:NE], ALU.subtract))
                assert step[0] == k0 + ROUTE_STEPS
                for c in range(NC):
                    for j in range(NPAIR):
                        k = (i * NC + c) * NPAIR + j
                        dve.wait_ge(m_sg, k + 1)
                        if k >= 2:
                            if j != 1:
                                dve.wait_ge(m_y, ((k - 2) // NPAIR) * (NPAIR - 1) + (k - 2) % NPAIR + 1)
                            else:
                                dve.wait_ge(s_lin, outputs((U_M0, U_M1)[i], c - 1))
                        nc.vector.tensor_tensor(moe[:, 1, k % 2], bank(2 + k % 2), moe[:, 0, k % 2], ALU.mult)\
                            .then_inc(m_su, 1)
                        dve.wait_ge(m_su, k + 1)
                        nc.vector.tensor_tensor(moe[:, 2, k % 2], bank(spread_bank(c, j)), moe[:, 1, k % 2],
                                                ALU.mult).then_inc(m_h, 1)
                        if c and j == 1:
                            dve.wait_ge(e_x, NC * i + c)
                            residual(U_M0 if i == 0 else U_M1, x, c - 1)
                dve.wait_ge(e_x, NC * i + NC)
                residual(U_M0 if i == 0 else U_M1, x, NC - 1)

            norm(0)
            project(AW)
            for k in range(2):
                dve.wait_ge(s_fa, k + 1)
                nc.vector.tensor_copy(nsq[:, k, 0:128], ps[:, k, 0:128]).then_inc(s_fb, 1)
            dve.wait_ge(s_fa, 3)
            nc.vector.tensor_copy(fm[:], ps[:, 2, 0:128]).then_inc(s_fb, 1)
            dve.wait_ge(s_fa, 4)
            nc.vector.tensor_copy(g_kv[:], ps[:, 3, 0:96]).then_inc(s_fb, 1)
            dve.wait_ge(s_w, 16)
            nc.vector.tensor_tensor(w_("sf_w"), w_("sf_w"), w_("sf_m"), ALU.mult).then_inc(s_fb, 1)
            attention_loop(AW)
            attention_end(AW, U_AW, x)
            norm(1)
            for c in range(NC):
                residual(U_F0, x, c, "f_b")
            norm(2)
            norm(3)
            project(AG)
            attention_loop(AG)
            attention_end(AG, U_AG, h)
            norm(4)
            project(AL)
            attention_loop(AL)
            attention_end(AL, U_AL, h)
            norm(5)
            for c in range(NC):
                residual(U_F1, x, c, "f_b")
            norm(6)
            for c in range(NC):
                dve.wait_ge(l_tr, c + 1)
                nc.vector.tensor_copy(zr[:, 4 * c:4 * c + 4, :].rearrange("p t d -> p (t d)"), bank(4 + c))\
                    .then_inc(l_tc, 1)
            near = c_("near")
            for v in range(B * KT + 1):
                if v < B * KT:
                    t = v % KT
                    dve.wait_ge(l_s, v + 1)
                    if v >= 2:
                        dve.wait_ge(l_th, v - 1)
                    nc.vector.tensor_tensor(work[:, (v % 2) * S:(v % 2 + 1) * S], two(2 * (v % 2)),
                                            near[:, P * (KT - 1 - t):P * (KT - 1 - t) + S], ALU.mult)\
                        .then_inc(l_w, 1)
                if v:
                    u = v - 1
                    b = u // KT
                    acc = dacc[:, b * S:(b + 1) * S]
                    wt = work[:, (4 + u % 2) * S:(5 + u % 2) * S]
                    dve.wait_ge(l_p, u + 1)
                    if u % KT == 0:
                        nc.vector.tensor_copy(acc, wt).then_inc(l_acc, 1)
                    else:
                        dve.wait_ge(l_acc, u)
                        nc.vector.tensor_tensor(acc, acc, wt, ALU.add).then_inc(l_acc, 1)
            for c in range(NC):
                dve.wait_ge(l_den, c + 1)
                nc.vector.tensor_scalar(ch(dloc, c), bank(c), 1e-7, None, ALU.add).then_inc(d_add, 1)
            for c in range(NC):
                k = 4 * R_LOC + c
                dve.wait_ge(d_u, k + 1)
                nc.vector.scalar_tensor_tensor(out=rcp[:, 2, c], in0=rcp[:, 1, c], scalar=-2.0,
                                               in1=rcp[:, 0, c], op0=ALU.add, op1=ALU.mult).then_inc(d_v, 1)
                dve.wait_ge(d_v, k + 1)
                dve.wait_ge(l_pv, B * KT)
                nc.vector.scalar_tensor_tensor(out=rcp[:, 2, c], in0=bank(4 + c), scalar=-1.0,
                                               in1=rcp[:, 2, c], op0=ALU.mult, op1=ALU.mult).then_inc(d_o, 1)
                dve.wait_ge(d_o, k + 1)
                nc.vector.tensor_tensor(ch(x, c), ch(x, c), rcp[:, 2, c], ALU.add).then_inc(s_res, 1)
            norm(7)
            moe_layer(0)
            norm(8)
            norm(9)
            for c in range(NC):
                residual(U_SF, h, c, "sf_b")
            norm(10)
            project(AR)
            attention_loop(AR)
            attention_end(AR, U_AR, h, "r_bo")
            norm(11)
            for c in range(NC):
                residual(U_FF, h, c, "ff2_b")
            norm(12)
            moe_layer(1)

        @block.tensor
        def _(pe):
            def mm(o, l, r, start=True, stop=True):
                return nc.tensor.matmul(o, l, r, start=start, stop=stop, skip_group_check=True)

            def norm(n):
                src, _, kind, _, _, _ = nrm(n)
                if kind == "ln":
                    for c in range(NC):
                        wait_source(pe, n, c)
                        mm(bank(c), c_("center"), ch(src, c)).then_inc(n_cen, 1)
                for c in range(NC):
                    pe.wait_ge(n_sq, 4 * n + c + 1)
                    mm(bank(4 + c), c_("mean"), nsq[:, c]).then_inc(n_var, 1)

            def project(a):
                n = N_OF[a]
                if a == AW:
                    wq, wk, wv = [(w_("a_wq"),)], [(w_("a_wk"),)], w_("a_wv")
                if a == AR:
                    wq, wk, wv = [(w_("r_wq"),)], [(w_("r_wk"),)], w_("r_wv")
                if a == AG:
                    wq, wk, wv = [(w_("g_wq"), w_("g_wqr"))], [(g_kv[:, 0:32], g_kv[:, 32:64])], g_kv[:, 64:96]
                if a == AL:
                    wq, wk, wv = [(w_("l_wq"), w_("l_wqr"))], [(w_("l_wk"), w_("l_wkr"))], w_("l_wv")
                r_v = KVH * D if GQA[a] else P

                def values_by_token(c):
                    if ROPE[a]:
                        if c < 2:
                            pe.wait_ge(n_z, 4 * n + 3 + c)
                        else:
                            pe.wait_ge(p_vf, 4 * a + c - 1)
                    else:
                        pe.wait_ge(p_f, (8 if a == AR else 0) + 2 * c + 1)
                    for tt in range(4):
                        ins = mm(bank(6 + c % 2 if ROPE[a] else c)[:, tt * r_v:(tt + 1) * r_v],
                                 z[:, (4 * c + tt) * P:(4 * c + tt + 1) * P], wv)
                    ins.then_inc(p_v, 1)

                for m in range(2 * NC + 1):
                    c, t = m // 2, m % 2
                    kr = 8 * a + m - 8
                    if m < 2 * NC:
                        if t == 0:
                            pe.wait_ge(n_z, 4 * n + c + 1)
                        ws = (wk if t else wq)[0]
                        if ROPE[a]:
                            r = KVH * D if t else P
                            if m >= 3:
                                pe.wait_ge(p_ln, kr - 2)
                            mm(ps[0:r, 2 * (m % 3), :], ws[0], ch(z, c))
                            mm(ps[0:r, 2 * (m % 3) + 1, :], ws[1], ch(z, c)).then_inc(p_mm, 1)
                        else:
                            mm(bank(c + 4 * t), ws[0], ch(z, c)).then_inc(p_mm, 1)
                    if m and t == 0:
                        values_by_token(c - 1)
                    if m and ROPE[a]:
                        u, tu = m - 1, (m - 1) % 2
                        r = KVH * D if tu else P
                        pe.wait_ge(p_sq, kr)
                        mm(ps[0:r, 2 * (u % 3), :], c_("head_k", r) if tu else c_("head_q"), rope_t[0:r, tu, 1])\
                            .then_inc(p_var, 1)

            def start_loop(a):
                q = A[a]
                for s in q["pv"]:
                    pe.sem_inc(s, 1)
                pe.wait_ge(p_vf, 4 * (a + 1))
                pe.wait_ge(p_2, 8 * (a + 1))

            def band_loop(a):
                q = A[a]
                w = W_A if a == AW else W_L
                mask = b_("band_a") if a == AW else b_("band_l")
                start_loop(a)

                def max_unit(g, b, k):
                    if k == 0:
                        pe.wait_ge(q["stack"][b], 96 * (g + 1))
                    g4, j0 = k // 4, 2 * (k % 4)
                    pe.wait_ge(w_m[k % 2], (16 + 2 * (1 - k % 2)) * g + (8 + 1 - k % 2) * b + k // 2 + 1)
                    mm(bank(4 + k % 2)[:, 0:2 * W_A], b_("ident"), b_("band_q"), True, False)
                    for j in range(2):
                        t = j0 + j
                        ins = mm(bank(4 + k % 2)[:, j * W_A:(j + 1) * W_A], qst[:, b, g4, t * P:(t + 1) * P],
                                 kst[:, b, g4, t * P:t * P + W_A], False, j == 1)
                    ins.then_inc(w_s[k % 2], 1)

                def transposed_maxima(g, b):
                    pe.wait_ge(w_m[0], 18 * g + 9 * b + 8 + 1)
                    pe.wait_ge(w_m[1], 16 * g + 8 * b + 8 + 1)
                    nc.tensor.transpose(bank(4)[0:G * KT, 0:P], mxq[:, b, :], c_("ident")).then_inc(w_t, 1)

                def score_unit(g, b, k):
                    st, g4 = k // G, k % G
                    kg = 0 if GQA[a] else g4
                    pe.wait_ge(q["soft"][k % 2], 8 * g + 4 * b + k // 2 + 1)
                    for half in range(2):
                        o = bank(2 * (k % 2) + half)
                        mm(o[:, 0:2 * w], b_("ident"), mask, True, False)
                        for j in range(2):
                            t = 4 * st + 2 * half + j
                            wt = min(w, S - t * P)
                            ins = mm(o[:, j * w:j * w + wt], kst[:, b, kg, PAD + t * P:PAD + (t + 1) * P],
                                     qst[:, b, g4, t * P:t * P + wt], False, j == 1)
                    ins.then_inc(q["unit"][k % 2], 1)

                def values(g, b, st):
                    for g4 in range(G):
                        k = G * st + g4
                        pe.wait_ge(q["soft"][k % 2], 8 * g + 4 * b + k // 2 + 2)
                    if st == 0:
                        pe.wait_ge(q["vg"][b], g + 1)
                        pe.wait_ge(q["oev"][1 - b], g + 1 + b)
                    for j in range(4):
                        t = 4 * st + j
                        cuts = [(t * P, min(t * P + w, (t // 4 + 1) * CH))]
                        if t == 3:
                            cuts.append((CH, t * P + w))
                        for lo, hi in cuts:
                            for g4 in range(G):
                                kg = 0 if GQA[a] else g4
                                ins = mm(two(6)[32 * g4:32 * g4 + VW, lo:hi], vg[:, b, t, kg, :],
                                         prob[:, st, g4].rearrange("p (a s) -> p a s", a=2)
                                         [:, j // 2, (j % 2) * w + lo - t * P:(j % 2) * w + hi - t * P],
                                         lo in (0, CH) and t in (0, 3), t == KT - 1)
                    ins.then_inc(q["pv"][st], 1)

                def body(g, last):
                    for b in range(B):
                        if a == AW:
                            pe.wait_ge(w_l[b], 48 * (g + 1))
                        else:
                            pe.wait_ge(q["stack"][b], 64 * (g + 1))
                        nxt = (g + (b + 1) // B, (b + 1) % B)
                        ahead = a == AW and not (last and b == B - 1)
                        k_max = 0
                        for k in range(2 * G):
                            score_unit(g, b, k)
                            for _ in range(MAX_AFTER[k] if ahead else 0):
                                max_unit(*nxt, k_max)
                                k_max += 1
                        if ahead:
                            transposed_maxima(*nxt)
                        values(g, b, 0)
                        values(g, b, 1)

                if a == AW:
                    for k in range(16):
                        max_unit(0, 0, k)
                    transposed_maxima(0, 0)
                    with pe.Fori(0, NG - 1) as g:
                        body(g, False)
                    body(NG - 1, True)
                else:
                    with pe.Fori(0, NG) as g:
                        body(g, False)

            def full_loop(a):
                q = A[a]
                start_loop(a)

                def scores(g, b, st):
                    for g4 in range(G):
                        k = G * st + (g4 if st < 5 else 0)
                        kg = 0 if GQA[a] else g4
                        if st < 5 or g4 == 0:
                            pe.wait_ge(q["soft"][k % 3], 14 * g + 7 * b + k // 3 + 1)
                        o = two(2 * (k % 3))
                        for t, q0, lo, hi in reversed(pieces(st, g4)):
                            mm(o[:, lo:hi], kst[:, b, kg, PAD + t * P:PAD + (t + 1) * P],
                               qst[:, b, g4, q0:q0 + hi - lo], True, q0 != t * P)
                            if q0 == t * P:
                                ins = mm(o[:, lo:lo + P], b_("ident"), b_("causal"), False, True)
                        if st < 5 or g4 == G - 1:
                            ins.then_inc(q["unit"][k % 3], 1)

                def values(g, b, st):
                    for g4 in range(G if st < 5 else 1):
                        k = G * st + g4
                        pe.wait_ge(q["soft"][k % 3], 14 * g + 7 * b + k // 3 + 2)
                    if st == 0:
                        pe.wait_ge(q["vg"][b], g + 1)
                        pe.wait_ge(q["oev"][1 - b], g + 1 + b)
                    for n in range(len(pieces(st, 0))):
                        for g4 in range(G):
                            t, q0, lo, hi = pieces(st, g4)[n]
                            kg = 0 if GQA[a] else g4
                            pb = prob[:, st % 2, g4 if st < 5 else 0]
                            ins = mm(two(6)[32 * g4:32 * g4 + VW, q0:q0 + hi - lo], vg[:, b, t, kg, :],
                                     pb[:, lo:hi], t == 0, t == KT - 1)
                    ins.then_inc(q["pv"][st % 2], 1)

                def body(g, last):
                    for b in range(B):
                        if a == AR:
                            pe.wait_ge(q["stack"][b], 64 * (g + 1))
                            scores(g, b, 0)
                        for st in range(STEPS):
                            if st + 1 < STEPS:
                                scores(g, b, st + 1)
                            elif a == AG and not (last and b == B - 1):
                                g_n, b_n = g + (b + 1) // B, (b + 1) % B
                                pe.wait_ge(q["stack"][b_n], 64 * (g_n + 1))
                                scores(g_n, b_n, 0)
                            values(g, b, st)

                if a == AR:
                    with pe.Fori(0, NG) as g:
                        body(g, False)
                    return
                pe.wait_ge(q["stack"][0], 64)
                scores(0, 0, 0)
                with pe.Fori(0, NG - 1) as g:
                    body(g, False)
                body(NG - 1, True)

            def attention_end(a, u, wo):
                i = RECIP_OF[a]
                for c in range(NC):
                    pe.wait_ge(d_o, 4 * i + c + 1)
                    mm(bank(4 + c), w_(wo), ch(ot, c)).then_inc(s_lin, 1)

            def linear(u, n, lhs):
                for c in range(NC):
                    pe.wait_ge(n_z, 4 * n + c + 1)
                    mm(bank(4 + c), lhs, ch(z, c)).then_inc(s_lin, 1)

            def moe_layer(i, n):
                pe.wait_ge(n_z, 4 * n + NC)
                for t in range(T // P):
                    ins = mm(bank(7)[:, t * NE:(t + 1) * NE], z[:, t * P:(t + 1) * P], w_("gate_w"))
                ins.then_inc(m_log, 1)
                wg, wu = [w_(name)[:, NPAIR * P:NPAIR * P + INTER] for name in ("w_gate", "w_up")]
                wd = w_("w_down", INTER)[:, NPAIR * P:NPAIR * P + P]
                for c in range(NC + 1):
                    k = NC * i + c
                    if c < NC:
                        if c >= 2:
                            pe.wait_ge(e_a, k - 1)
                        mm(ps[0:INTER, c % 2, :], wg, ch(z, c))
                        mm(ps[0:INTER, 2 + c % 2, :], wu, ch(z, c)).then_inc(e_gu, 1)
                    if c:
                        pe.wait_ge(e_m, k)
                        if c == NC:
                            pe.wait_ge(m_e, i + 1)
                        mm(bank(4 + c - 1), wd, moe[0:INTER, 5, (c - 1) % 2]).then_inc(e_y, 1)
                pe.wait_ge(e_a, NC * (i + 1))

                def gate_up(c, j):
                    k = (i * NC + c) * NPAIR + j
                    if k >= 2:
                        pe.wait_ge(m_su, k - 1)
                    mm(bank(k % 2), w_("w_gate")[:, j * P:(j + 1) * P], ch(z, c))
                    mm(bank(2 + k % 2), w_("w_up")[:, j * P:(j + 1) * P], ch(z, c))

                def spread(c, j):
                    k = (i * NC + c) * NPAIR + j
                    if k - 1 > i * NC * NPAIR:
                        pe.wait_ge(m_h, k - 1)
                    mm(bank(spread_bank(c, j)), b_("spread")[:, j * P:(j + 1) * P], ch(comb, c)).then_inc(m_gu, 1)

                def down(c, j):
                    k = (i * NC + c) * NPAIR + j
                    pe.wait_ge(m_h, k + 1)
                    return mm(bank(4 + c), w_("w_down")[:, j * P:(j + 1) * P], moe[:, 2, k % 2], j == 0, j == NPAIR - 1)

                gate_up(0, 0)
                pe.wait_ge(m_d, ROUTE_STEPS * (i + 1))
                pe.wait_ge(e_o, NC * (i + 1))
                for c in range(NC):
                    for tt in range(4):
                        ins = mm(bank(4 + c)[0:96, tt * P:(tt + 1) * P],
                                 cparts[:, 4 * c + tt].rearrange("p i e -> p (i e)"), b_("ident"))
                    ins.then_inc(m_t, 1)
                pe.wait_ge(m_cs, NC * (i + 1))
                spread(0, 0)
                todo = [(c, j) for c in range(NC) for j in range(NPAIR)]
                for n_, (c, j) in enumerate(todo):
                    if n_ + 1 < len(todo):
                        gate_up(*todo[n_ + 1])
                        spread(*todo[n_ + 1])
                    down(c, j).then_inc(m_y if j < NPAIR - 1 else s_lin, 1)

            pe.wait_ge(s_nc, 16)
            pe.wait_ge(s_set, 4)
            norm(0)
            pe.wait_ge(s_w0, 16)
            project(AW)
            pe.wait_ge(p_vf, NC)
            pe.wait_ge(s_cst, 48)
            pe.wait_ge(s_w, 16)
            mm(ps[:, 0, 0:128], w_("f_re"), c_("dft_c"), True, False)
            mm(ps[:, 0, 0:128], w_("f_im"), c_("dft_s"), False, True).then_inc(s_fa, 1)
            mm(ps[:, 1, 0:128], w_("f_im"), c_("dft_c"), True, False)
            mm(ps[:, 1, 0:128], w_("f_re"), c_("dft_ns"), False, True).then_inc(s_fa, 1)
            pe.wait_ge(s_fb, 2)
            mm(ps[:, 2, 0:128], nsq[:, 0, 0:128], c_("idft_c"), True, False)
            mm(ps[:, 2, 0:128], nsq[:, 1, 0:128], c_("idft_ns"), False, True).then_inc(s_fa, 1)
            a0 = WAT["g_kup"][0]
            mm(ps[:, 3, 0:96], w_("g_kvd", 32), wsb[0:32, a0:a0 + 96]).then_inc(s_fa, 1)
            pe.wait_ge(s_fb, 5)
            band_loop(AW)
            attention_end(AW, U_AW, "a_wo")
            norm(1)
            linear(U_F0, 1, fm[:])
            norm(2)
            norm(3)
            project(AG)
            full_loop(AG)
            attention_end(AG, U_AG, "g_wo")
            norm(4)
            project(AL)
            band_loop(AL)
            attention_end(AL, U_AL, "l_wo")
            norm(5)
            linear(U_F1, 5, fm[:])
            norm(6)
            for c in range(NC):
                pe.wait_ge(n_z, 4 * 6 + c + 1)
                mm(bank(c), w_("loc_w"), ch(z, c)).then_inc(l_xt, 1)
                for tt in range(4):
                    t = 4 * c + tt
                    ins = nc.tensor.transpose(bank(4 + c)[:, tt * P:(tt + 1) * P], z[:, t * P:(t + 1) * P],
                                              c_("ident"))
                ins.then_inc(l_tr, 1)
            pe.wait_ge(l_xc, NC)
            pe.wait_ge(l_tc, NC)
            for v in range(B * KT + 1):
                if v < B * KT:
                    b = v // KT
                    if v >= 2:
                        pe.wait_ge(l_w, v - 1)
                    for half in range(2):
                        ins = mm(bank(2 * (v % 2) + half), z[:, v * P:(v + 1) * P], ch(xtr, CB * b + half))
                    ins.then_inc(l_s, 1)
                if v:
                    u = v - 1
                    b = u // KT
                    pe.wait_ge(l_p, u + 1)
                    for half in range(2):
                        ins = mm(bank(4 + CB * b + half), zr[:, u, :],
                                 work[:, (4 + u % 2) * S + half * CH:(4 + u % 2) * S + (half + 1) * CH],
                                 u % KT == 0, u % KT == KT - 1)
                    ins.then_inc(l_pv, 1)
            for c in range(NC):
                if c == 0:
                    pe.wait_ge(l_acc, B * KT)
                    pe.wait_ge(l_w, B * KT)
                mm(bank(c), c_("ones"), ch(dacc, c)).then_inc(l_den, 1)
            norm(7)
            moe_layer(0, 7)
            norm(8)
            norm(9)
            linear(U_SF, 9, w_("sf_w"))
            norm(10)
            project(AR)
            full_loop(AR)
            attention_end(AR, U_AR, "r_wo")
            norm(11)
            for c in range(NC):
                pe.wait_ge(n_z, 4 * 11 + c + 1)
                for j in range(FF // P):
                    if c:
                        pe.wait_ge(f_r, 4 * (c - 1) + j + 1)
                    elif j:
                        pe.wait_ge(n_z, 4 * 11 + j + 1)
                    mm(bank(j), w_("ff1")[:, j * P:(j + 1) * P], ch(z, c)).then_inc(f_h, 1)
                for j in range(FF // P):
                    pe.wait_ge(f_r, 4 * c + j + 1)
                    ins = mm(bank(4 + c), w_("ff2")[:, j * P:(j + 1) * P], ffh[:, c % 2, j], j == 0, j == 3)
                ins.then_inc(s_lin, 1)
            norm(12)
            moe_layer(1, 12)



def bf16_parts(v):
    out, rest = [], v.astype(np.float32)
    for _ in range(3):
        part = rest.astype(BF16_NP)
        out.append(part)
        rest = rest - part.astype(np.float32)
    return out


def float_constants():
    c = np.zeros((P, CN), np.float32)

    def put(name, v):
        a, b = CAT[name]
        c[0:v.shape[0], a:b] = v

    i = np.arange(P)
    ang = 2.0 * np.pi * ((i[:, None] * i[None, :]) % P) / P
    put("dft_c", np.cos(ang))
    put("dft_s", np.sin(ang))
    put("dft_ns", -np.sin(ang))
    put("idft_c", np.cos(ang) / P)
    put("idft_ns", -np.sin(ang) / P)
    put("ident", np.eye(P))
    put("center", np.eye(P) - 1.0 / P)
    put("mean", np.full((P, P), 1.0 / P))
    put("ones", np.ones((P, P)))
    head = i // (D * G) * G + i % G
    put("head_q", (head[:, None] == head[None, :]) / D)
    j = np.arange(KVH * D)
    put("head_k", (j[:, None] % KVH == j[None, :] % KVH) / D)
    put("offdiag", 1.0 - np.eye(P))
    dist = np.abs(np.arange(P * (2 * KT - 1))[None, :] - P * (KT - 1) - i[:, None]).astype(np.float32)
    near = np.float32(1.0) / (dist + np.float32(1e-7)) * (dist != 0).astype(np.float32)
    put("near", near)
    return c


def bfloat_constants():
    c = np.zeros((P, BN), np.float32)

    def put(name, v):
        a, b = BAT[name]
        c[0:v.shape[0], a:b] = v

    i = np.arange(P)[:, None]
    put("ident", np.eye(P))
    w = np.arange(W_A)[None, :]
    ok = (i - w + PAD >= 0) & (i - w + PAD <= WIN_A)
    put("band_q", np.tile(np.where(ok, 0.0, NEG), (1, 2)))
    ok = (w - i >= 0) & (w - i <= WIN_A)
    put("band_a", np.tile(np.where(ok, 0.0, NEG), (1, 2)))
    w = np.arange(W_L)[None, :]
    ok = (w - i >= 0) & (w - i < WIN_L)
    put("band_l", np.tile(np.where(ok, 0.0, NEG), (1, 2)))
    put("causal", np.where(np.arange(P)[None, :] >= i, 0.0, NEG))
    spread = np.zeros((P, NPAIR, 2, INTER), np.float32)
    for e in range(NE):
        for part in range(3):
            spread[32 * part + e, e // 2, e % 2, :] = 1.0
    put("spread", spread.reshape(P, -1))
    return c.astype(BF16_NP)


def rope_tables():
    q = np.zeros((2, 2, P, S), np.float32)
    k = np.zeros((2, 2, KVH * D, S), np.float32)
    for n, base in enumerate((1000000.0, 10000.0)):
        inv = np.float32(1.0) / np.float32(base) ** (np.arange(0, D, 2, dtype=np.float32) / np.float32(D))
        f = np.arange(S, dtype=np.float32)[:, None] * inv.astype(np.float32)[None, :]
        cos, sin = np.cos(f).astype(np.float32), np.sin(f).astype(np.float32)
        for d in range(D):
            sg = -1.0 if d % 2 == 0 else 1.0
            for g in range(NG):
                row = (g * D + d) * G
                q[n, 0, row:row + G] = cos[:, d // 2]
                q[n, 1, row:row + G] = sg * sin[:, d // 2]
            k[n, 0, d * KVH:(d + 1) * KVH] = cos[:, d // 2]
            k[n, 1, d * KVH:(d + 1) * KVH] = sg * sin[:, d // 2]
    return q, k


def window_bias():
    slope = np.exp2(-(np.arange(H, dtype=np.float32) + 1.0) * 8.0 / H).astype(np.float32)
    c = bf16_parts(slope * np.sqrt(np.float32(D)))
    q = np.zeros((XROWS, H, S), np.float32)
    k = np.zeros((XROWS, H, SL), np.float32)
    t = np.arange(S)
    lo, odd = t % P, (t // P) % 2
    for i in range(3):
        ci = c[i].astype(np.float32)[:, None]
        q[i], k[i, :, PAD:] = lo[None], ci
        q[3 + i], k[3 + i, :, PAD:] = ci, -lo[None]
        q[6 + i], k[6 + i, :, PAD:] = P * odd[None], ci * (1 - odd)[None]
        q[9 + i], k[9 + i, :, PAD:] = P * (1 - odd)[None], ci * odd[None]
    q[12] = 1.0
    k[12, :, 0:PAD] = NEG
    k[13:16, :, PAD:] = 1.0
    return q.astype(BF16_NP), k.astype(BF16_NP)



def kernel(**inputs):
    import concourse.bacc as _bacc
    from concourse.bass_utils import run_bass_kernel_spmd as _run

    v = {k: np.ascontiguousarray(a) for k, a in inputs.items()}
    pq = np.array([(g * G + hd) * D + d for g in range(NG) for d in range(D) for hd in range(G)])
    pqr = np.array([(g * G + hd) * D + (d ^ 1) for g in range(NG) for d in range(D) for hd in range(G)])
    pk = np.array([hd * D + d for d in range(D) for hd in range(KVH)])
    pkr = np.array([hd * D + (d ^ 1) for d in range(D) for hd in range(KVH)])

    w = np.zeros((P, WN), np.float32)

    def put(name, a):
        lo, hi = WAT[name]
        w[0:a.shape[0], lo:hi] = a

    w_in = v["L0_attn_a_w_in"].T
    put("a_wq", w_in[:, 0:E][:, pq])
    put("a_wk", w_in[:, E:2 * E][:, pq])
    put("a_wv", w_in[:, 2 * E:])
    put("a_wo", v["L0_attn_a_w_out"].T)
    put("g_wq", v["L0_attn_b_g_wq"][:, pq])
    put("g_wqr", v["L0_attn_b_g_wq"][:, pqr])
    put("g_wo", v["L0_attn_b_g_wo"])
    put("g_kvd", v["L0_attn_b_g_kv_down"].T)
    put("g_kup", v["L0_attn_b_g_k_up"][:, pk])
    put("g_kupr", v["L0_attn_b_g_k_up"][:, pkr])
    put("g_vup", v["L0_attn_b_g_v_up"])
    put("l_wq", v["L0_attn_b_l_wq"][:, pq])
    put("l_wqr", v["L0_attn_b_l_wq"][:, pqr])
    put("l_wk", v["L0_attn_b_l_wk"][:, pk])
    put("l_wkr", v["L0_attn_b_l_wk"][:, pkr])
    put("l_wv", v["L0_attn_b_l_wv"])
    put("l_wo", v["L0_attn_b_l_wo"])
    put("f_re", v["L0_ffn_w_freq_real"])
    put("f_im", v["L0_ffn_w_freq_imag"])
    put("loc_w", v["L1_attn_a_W"])
    put("sf_w", v["L1_attn_b_sf_w"].T)
    put("sf_m", v["L1_attn_b_mask"].T)
    put("r_wq", v["L1_attn_b_wq"].T[:, pq])
    put("r_wk", v["L1_attn_b_wk"].T[:, pq])
    put("r_wv", v["L1_attn_b_wv"].T)
    put("r_wo", v["L1_attn_b_wo"].T)
    put("r_bv", np.broadcast_to(v["L1_attn_b_bv"][None, :], (P, E)))
    put("ff1", v["L1_attn_b_ff1_w"].T)
    put("ff2", v["L1_attn_b_ff2_w"].T.reshape(FF // P, P, E).transpose(1, 0, 2).reshape(P, FF))
    put("gate_w", v["L1_ffn_gate_w"].T)
    put("gate_b", np.broadcast_to(v["L1_ffn_gate_b"][None, :], (P, NE)))
    w13 = v["L1_ffn_w13"].transpose(2, 0, 1)
    put("w_gate", np.concatenate([w13[:, :, 0:INTER].reshape(P, -1), v["L1_ffn_w13_s"].T[:, 0:INTER]], axis=1))
    put("w_up", np.concatenate([w13[:, :, INTER:].reshape(P, -1), v["L1_ffn_w13_s"].T[:, INTER:]], axis=1))
    lo, hi = WAT["w_down"]
    w[:, lo:hi - P] = v["L1_ffn_w2"].transpose(0, 2, 1).reshape(NPAIR, P, E).transpose(1, 0, 2).reshape(P, -1)
    w[0:INTER, hi - P:hi] = v["L1_ffn_w2_s"].T
    vec = np.zeros((P, len(VCOLS)), np.float32)
    names = {"n1": "L0_attn_b_norm1_w", "n2": "L0_attn_b_norm2_w", "f_b": "L0_ffn_bias", "loc_b": "L1_attn_a_b",
             "sf_b": "L1_attn_b_sf_b", "r_bo": "L1_attn_b_bo", "ff2_b": "L1_attn_b_ff2_b"}
    names.update({n: f"L1_attn_b_{n}" for n in ("g1", "b1", "g2", "b2", "g3", "b3")})
    for n, full in names.items():
        vec[:, VAT[n]] = v[full]
    vec[:, VAT["r_bq"]] = v["L1_attn_b_bq"][pq]
    vec[:, VAT["r_bk"]] = v["L1_attn_b_bk"][pq]
    for j in range(FF // P):
        vec[:, VAT[f"ff1_b{j}"]] = v["L1_attn_b_ff1_b"][j * P:(j + 1) * P]

    rq, rk = rope_tables()
    bq, bk = window_bias()
    arrays = {
        "in_x": np.ascontiguousarray(v["L0_attn_a_x"].reshape(T, E).T), "in_w": w, "in_v": vec,
        "in_c": float_constants(), "in_b": bfloat_constants(), "in_rq": rq, "in_rk": rk, "in_bq": bq, "in_bk": bk,
    }
    nc = _bacc.Bacc("TRN2", target_bir_lowering=False, num_devices=1)
    args = [nc.dram_tensor(n, a.shape, mybir.dt.from_np(a.dtype), kind="ExternalInput").ap()
            for n, a in arrays.items()]
    args.append(nc.dram_tensor("out_x", (E, T), F32, kind="ExternalOutput").ap())
    build(nc, *args)
    r = _run(nc, [arrays], core_ids=[0])
    return np.ascontiguousarray(r.results[0]["out_x"].T).reshape(B, S, E)
```
